# Optimizing a Trainium2 kernel written in Bass

```python
import numpy as np
import jax
import jax.numpy as jnp

def _softmax(x, axis=-1):
    return jax.nn.softmax(x, axis=axis)

def _gelu(x):
    return jax.nn.gelu(x, approximate=True)

def _silu(x):
    return jax.nn.silu(x)

def _sigmoid(x):
    return jax.nn.sigmoid(x)

def _layernorm(x, axis=-1, eps=1e-05):
    m = jnp.mean(x, axis=axis, keepdims=True)
    v = jnp.var(x, axis=axis, keepdims=True)
    return (x - m) / jnp.sqrt(v + eps)

def _scatter_add(tgt, idx, src, axis=0):
    return tgt.at[idx].add(src)

def _segment_sum(src, seg, n):
    return jax.ops.segment_sum(src, seg, n)
kernel_name = 'mk_flamingo_gated_d1_seqx_r8_227d4f'

def setup_inputs(seed: int=0):
    np.random.seed(seed)
    _w = jnp.asarray

    def _rec_inputs():
        import jax
        import jax.numpy as jnp
        _rk = jax.random.key(seed)
        x = -0.0002928 + 1 * jax.random.normal(jax.random.fold_in(_rk, 1), (8, 256, 128), jnp.float32)
        _lenS = 256 - jax.random.randint(jax.random.fold_in(_rk, 7), (8,), 0, max(1, 256 // 4) + 1, jnp.int32)
        _lenS2 = 256 - jax.random.randint(jax.random.fold_in(_rk, 8), (8,), 0, max(1, 256 // 4) + 1, jnp.int32)
        _ctx_1024P = jax.random.normal(jax.random.fold_in(_rk, 11), (8, 16, 128), jnp.float32)
        _ctx_1024c = jax.random.dirichlet(jax.random.fold_in(_rk, 511), 0.3 * jnp.ones((16,), jnp.float32), (8, 256))
        _ctx_1024t = jnp.einsum('bsk,bkd->bsd', _ctx_1024c, _ctx_1024P)
        _ctx_1024t = _ctx_1024t * jax.lax.rsqrt(jnp.mean(jnp.square(_ctx_1024t)) + 1e-12) * 0.953939
        ctx_1024 = -1.39393e-06 + 0.999914 * (_ctx_1024t + 0.3 * jax.random.normal(jax.random.fold_in(_rk, 611), (8, 256, 128), jnp.float32))
        _g = jax.random.normal(jax.random.fold_in(_rk, 9001), (2, 1), jnp.float32)
        _g = jnp.sign(_g) * jnp.maximum(jnp.abs(_g), 1.0) + (_g == 0) * 1.0
        g_xattn = _g[0]
        g_ffn = _g[1]
        return (x, ctx_1024, g_xattn, g_ffn)
    x, ctx_1024, g_xattn, g_ffn = _rec_inputs()

    def _L0_xattn_setup():
        import jax, jax.numpy as jnp
        import numpy as np
        H, DK, DV = (16, 64, 64)
        MEM = 128
        D_MODEL = 128
        OUT_DIM = 128
        key = jax.random.key(seed)
        ks = jax.random.split(key, 12)
        B, S = (2, 256)
        scale = 1.0 / np.sqrt(D_MODEL)
        inp = {'queries': jax.random.normal(ks[0], (B, S, D_MODEL), jnp.float32), 'keys': jax.random.normal(ks[1], (B, S, D_MODEL), jnp.float32), 'values': jax.random.normal(ks[2], (B, S, D_MODEL), jnp.float32), 'wq_w': jax.random.normal(ks[3], (D_MODEL, H * DK), jnp.float32) * scale, 'wq_b': jnp.zeros((H * DK,), jnp.float32), 'wk_w': jax.random.normal(ks[4], (D_MODEL, H * DK), jnp.float32) * scale, 'wk_b': jnp.zeros((H * DK,), jnp.float32), 'wv_w': jax.random.normal(ks[5], (D_MODEL, H * DV), jnp.float32) * scale, 'wv_b': jnp.zeros((H * DV,), jnp.float32), 'mk': jax.random.normal(ks[6], (1, MEM, H * DK), jnp.float32) * (0.1 / DK), 'mv': jax.random.normal(ks[7], (1, MEM, H * DV), jnp.float32) * (0.1 / MEM), 'wo_w': jax.random.normal(ks[8], (H * DV, OUT_DIM), jnp.float32) * (1.0 / np.sqrt(H * DV)), 'wo_b': jnp.zeros((OUT_DIM,), jnp.float32)}
        return inp
    _L0_xattn_all = _L0_xattn_setup()
    _L0_xattn_in = {k: v for k, v in _L0_xattn_all.items() if k in ('wq_w', 'wq_b', 'wk_w', 'wk_b', 'wv_w', 'wv_b', 'mk', 'mv', 'wo_w', 'wo_b')}
    del _L0_xattn_all

    def _L0_ffn_setup():
        import jax, jax.numpy as jnp
        import numpy as np
        B, S, D = (1, 256, 128)
        E, K, F = (8, 2, 176)
        NS = 2
        SCALE = 2.5

        def _swiglu_mlp(x, wg, wu, wd):
            return jax.nn.silu(x @ wg) * (x @ wu) @ wd
        key = jax.random.key(seed)
        ks = jax.random.split(key, 8)
        s = 0.02
        return {'hidden_states': jax.random.normal(ks[0], (B, S, D), jnp.float32), 'gate_w': jax.random.normal(ks[1], (E, D), jnp.float32) * s, 'w_gate': jax.random.normal(ks[2], (E, D, F), jnp.float32) * s, 'w_up': jax.random.normal(ks[3], (E, D, F), jnp.float32) * s, 'w_down': jax.random.normal(ks[4], (E, F, D), jnp.float32) * s, 'sw_gate': jax.random.normal(ks[5], (D, F * NS), jnp.float32) * s, 'sw_up': jax.random.normal(ks[6], (D, F * NS), jnp.float32) * s, 'sw_down': jax.random.normal(ks[7], (F * NS, D), jnp.float32) * s}
    _L0_ffn_all = _L0_ffn_setup()
    _L0_ffn_in = {k: v for k, v in _L0_ffn_all.items() if k in ('gate_w', 'w_gate', 'w_up', 'w_down', 'sw_gate', 'sw_up', 'sw_down')}
    del _L0_ffn_all
    return {'x': x, 'ctx_1024': ctx_1024, 'g_xattn': g_xattn, 'g_ffn': g_ffn, 'L0_xattn_wq_w': _L0_xattn_in['wq_w'], 'L0_xattn_wq_b': _L0_xattn_in['wq_b'], 'L0_xattn_wk_w': _L0_xattn_in['wk_w'], 'L0_xattn_wk_b': _L0_xattn_in['wk_b'], 'L0_xattn_wv_w': _L0_xattn_in['wv_w'], 'L0_xattn_wv_b': _L0_xattn_in['wv_b'], 'L0_xattn_mk': _L0_xattn_in['mk'], 'L0_xattn_mv': _L0_xattn_in['mv'], 'L0_xattn_wo_w': _L0_xattn_in['wo_w'], 'L0_xattn_wo_b': _L0_xattn_in['wo_b'], 'L0_ffn_gate_w': _L0_ffn_in['gate_w'], 'L0_ffn_w_gate': _L0_ffn_in['w_gate'], 'L0_ffn_w_up': _L0_ffn_in['w_up'], 'L0_ffn_w_down': _L0_ffn_in['w_down'], 'L0_ffn_sw_gate': _L0_ffn_in['sw_gate'], 'L0_ffn_sw_up': _L0_ffn_in['sw_up'], 'L0_ffn_sw_down': _L0_ffn_in['sw_down']}

def reference(x, ctx_1024, g_xattn, g_ffn, L0_xattn_wq_w, L0_xattn_wq_b, L0_xattn_wk_w, L0_xattn_wk_b, L0_xattn_wv_w, L0_xattn_wv_b, L0_xattn_mk, L0_xattn_mv, L0_xattn_wo_w, L0_xattn_wo_b, L0_ffn_gate_w, L0_ffn_w_gate, L0_ffn_w_up, L0_ffn_w_down, L0_ffn_sw_gate, L0_ffn_sw_up, L0_ffn_sw_down):
    import jax
    import jax.numpy as jnp

    def _L0_xattn_ref(queries, keys, values, wq_w, wq_b, wk_w, wk_b, wv_w, wv_b, mk, mv, wo_w, wo_b):
        import jax, jax.numpy as jnp
        import numpy as np
        H, DK, DV = (16, 64, 64)
        MEM = 128
        D_MODEL = 128
        OUT_DIM = 128
        B, S, _ = queries.shape
        q = (queries @ wq_w + wq_b).reshape(B, S, H, DK).transpose(0, 2, 1, 3)
        k_proj = keys @ wk_w + wk_b
        v_proj = values @ wv_w + wv_b
        k_ext = jnp.concatenate([k_proj, jnp.broadcast_to(mk, (B, MEM, H * DK))], axis=1)
        v_ext = jnp.concatenate([v_proj, jnp.broadcast_to(mv, (B, MEM, H * DV))], axis=1)
        T = S + MEM
        k = k_ext.reshape(B, T, H, DK).transpose(0, 2, 1, 3)
        v = v_ext.reshape(B, T, H, DV).transpose(0, 2, 1, 3)
        scores = jnp.einsum('bhsd,bhtd->bhst', q, k) / jnp.sqrt(jnp.float32(DK))
        attn = jax.nn.softmax(scores, axis=-1)
        out = jnp.einsum('bhst,bhtd->bhsd', attn, v)
        out = out.transpose(0, 2, 1, 3).reshape(B, S, H * DV)
        return out @ wo_w + wo_b

    def _L0_ffn_ref(hidden_states, gate_w, w_gate, w_up, w_down, sw_gate, sw_up, sw_down):
        import jax, jax.numpy as jnp
        import numpy as np
        B, S, D = (1, 256, 128)
        E, K, F = (8, 2, 176)
        NS = 2
        SCALE = 2.5

        def _swiglu_mlp(x, wg, wu, wd):
            return jax.nn.silu(x @ wg) * (x @ wu) @ wd
        identity = hidden_states
        x = hidden_states.reshape(-1, hidden_states.shape[-1])
        T = x.shape[0]
        logits = x.astype(jnp.float32) @ gate_w.astype(jnp.float32).T
        scores = jax.nn.softmax(logits, axis=-1)
        topk_w, topk_i = jax.lax.top_k(scores, K)
        topk_w = topk_w / (topk_w.sum(-1, keepdims=True) + 1e-20) * SCALE
        combine = jnp.zeros((T, E), jnp.float32).at[jnp.arange(T)[:, None], topk_i].set(topk_w)
        g = jax.nn.silu(jnp.einsum('td,edf->etf', x, w_gate)) * jnp.einsum('td,edf->etf', x, w_up)
        expert_out = jnp.einsum('etf,efd->etd', g, w_down)
        y = jnp.einsum('te,etd->td', combine, expert_out).astype(x.dtype)
        y = y.reshape(identity.shape)
        return y + _swiglu_mlp(identity, sw_gate, sw_up, sw_down)
    x = x + jnp.tanh(g_xattn[0]) * _L0_xattn_ref(_layernorm(x, axis=-1), ctx_1024, ctx_1024, L0_xattn_wq_w, L0_xattn_wq_b, L0_xattn_wk_w, L0_xattn_wk_b, L0_xattn_wv_w, L0_xattn_wv_b, L0_xattn_mk, L0_xattn_mv, L0_xattn_wo_w, L0_xattn_wo_b)
    x = x + jnp.tanh(g_ffn[0]) * _L0_ffn_ref(_layernorm(x, axis=-1), L0_ffn_gate_w, L0_ffn_w_gate, L0_ffn_w_up, L0_ffn_w_down, L0_ffn_sw_gate, L0_ffn_sw_up, L0_ffn_sw_down)
    return x

_drawn_inputs = setup_inputs


def setup_inputs(seed=0):
    import zlib

    import numpy as np

    out = dict(_drawn_inputs(seed))
    spreads = {'L0_xattn_wq_b': (0.0, 0.622),
     'L0_xattn_wk_b': (0.0, 0.8),
     'L0_xattn_wv_b': (0.0, 0.1),
     'L0_xattn_wo_b': (0.0, 0.1)}
    factors = {'L0_xattn_mk': 200.0,
     'L0_xattn_mv': 200.0,
     'L0_ffn_gate_w': 5.933,
     'L0_ffn_w_gate': 5.207,
     'L0_ffn_w_up': 5.175,
     'L0_ffn_w_down': 5.179,
     'L0_ffn_sw_gate': 6.572,
     'L0_ffn_sw_up': 6.529,
     'L0_ffn_sw_down': 6.553}
    for name, (base, spread) in spreads.items():
        noise = np.random.default_rng([zlib.crc32(name.encode()), seed]).standard_normal(out[name].shape)
        drawn = base * np.exp(spread * noise) if base else spread * noise
        out[name] = jnp.asarray(drawn.astype(out[name].dtype))
    for name, factor in factors.items():
        out[name] = (out[name] * factor).astype(out[name].dtype)
    return out
```

```python
import numpy as np

import concourse.bass as bass
from concourse import mybir
from contextlib import ExitStack

F32 = mybir.dt.float32
F32R = mybir.dt.float32r
BF16 = mybir.dt.bfloat16
U32 = mybir.dt.uint32
ALU = mybir.AluOpType
ACT = mybir.ActivationFunctionType
AX = mybir.AxisListType

P = 128
B, S, D = 8, 256, 128
TOK = B * S
H, DK = 16, 64
HD = H * DK
MEM = 128
T = S + MEM
BLK = 512
NBLK = TOK // BLK
NT = TOK // P
CH = BLK // P
BB = BLK // S
TC = T // P
NPAIR = H // 2
GH = 4
GW = GH * DK
NG = H // GH
E, FE = 8, 176
FS = 352
FEX = E * FE
FALL = FEX + FS
NJ = -(-FALL // P)
FPAD = NJ * P
NJE = FEX // P
LAST = FALL - (NJ - 1) * P
TOPK = 2
ROUTE_SCALE = 2.5
EPS = 1e-5
QSCALE = DK ** -0.5
PSLOT = 6
KW = S + MEM + S
PART = 32

assert FEX % P == 0 and BB == 2 and TC == 3


def flamingo_block(nc, x, ctx, g_xattn, g_ffn, wq, wq_b, wk, wk_b, wv, wv_b, mk, mv, wo, wo_b,
                   gate_w, w_gate, w_up, w_down, sw_gate, sw_up, sw_down, identity, selector, iota, out):
    with ExitStack() as es:
        def sb(name, shape, dt=F32):
            return es.enter_context(nc.sbuf_tensor(name, shape, dt))

        def sems(names):
            return {n: es.enter_context(nc.semaphore(n)) for n in names.split()}

        x_tok = sb("x_tok", [P, TOK])
        xT = sb("xT", [P, 2, TOK], F32R)
        cT = sb("cT", [P, 2, TOK], F32R)
        cT_blk = sb("cT_blk", [P, 2, BLK], F32R)
        wbig = sb("wbig", [P, 8 * HD], F32R)
        wvs = sb("wvs", [P, 2, HD], F32R)
        mem_k = sb("mem_k", [P, H, 2, MEM], F32R)
        mem_v = sb("mem_v", [P, HD])
        k_st = sb("k_st", [P, 2, 2, KW], F32R)
        q_st = sb("q_st", [P, 2, BLK], F32R)
        v_sb = sb("v_sb", [P, 2, CH, GW])
        bv_bc = sb("bv_bc", [P, HD])
        wo_sb = sb("wo_sb", [P, NPAIR, D])
        probs = sb("probs", [P, PSLOT, T])
        pT = sb("pT", [P, 4, BB, TC, S])
        oT = sb("oT", [P, 2, BLK])
        ffn_work = sb("ffn_work", [P, 2 * FPAD])
        wd_sb = sb("wd_sb", [P, NJ, D])
        sel_sb = sb("sel_sb", [P, NJE, P], BF16)
        cT_route = sb("cT_route", [P, TOK], BF16)
        ident = sb("ident", [P, P])
        ident_b = sb("ident_b", [P, P], BF16)
        iota_sb = sb("iota_sb", [P, E])
        brows = sb("brows", [H, 2, 2, DK])
        gw_row = sb("gw_row", [E, D])
        bq8 = sb("bq8", [P, H])
        bk = sb("bk", [P, H])
        gwT = sb("gwT", [P, 2, E], F32R)
        bo_col = sb("bo_col", [P, 1])
        gains = sb("gains", [P, 2])
        tg = sb("tg", [P, 2])
        stat = sb("stat", [P, NT, 6])
        mv_all = sb("mv_all", [P, NT, 2])
        std = sb("std", [P, NT])
        rstd = sb("rstd", [P, NT])
        nmax = sb("nmax", [P, PSLOT])
        psums = sb("psums", [P, PSLOT])
        rsum = sb("rsum", [P, PSLOT])

        wqk = wbig[:, :].rearrange("p (w s h r d) -> p w s h r d", w=2, s=2, h=H, r=2)
        gu_w = wbig[:, 0:4 * FPAD].rearrange("p (w s f) -> p w s f", w=2, s=2)
        stage = pT[:, :, :, :, :].rearrange("p a b c s -> p (a b c s)")
        raw_w = stage[:, 0:3 * HD].rearrange("p (w n) -> p w n", w=3)
        raw_mk = stage[:, 3 * HD:5 * HD].rearrange("p (h r d) -> p h r d", h=H, r=2)
        ctx_tok = ffn_work[:, 0:TOK]
        raw_gu = ffn_work[:, :].rearrange("p (w f) -> p w f", w=2)
        raw_sel = probs[:, :, :].rearrange("p a b -> p (a b)")[:, 0:NJE * P].rearrange("p (j f) -> p j f", j=NJE)
        xln = v_sb[:, :, :, :].rearrange("p a b c -> p (a b c)")

        banks = [es.enter_context(nc.psum_tensor(f"bank{i}", [P, 512], F32)) for i in range(8)]

        a = sems("x_in ctx_in wq_in wk_in wv_in mk_in mv_in bias_in gate_in gain_in ident_in bv_in wo_in bo_in "
                 "misc_in gu_in wd_in pad_done var_ready std_ready ln_ready ln_link tr_done hi_done lo_done "
                 "small_done small_copied wq_hi wk_hi wv_hi w_lo tanh_done gu_raw_free identb_done gw_hi gw_lo")
        NJOB = 3 * NBLK
        job_dst = ([cT[:, :, j * BLK:(j + 1) * BLK] for j in range(NBLK)]
                   + [mem_k[:, 4 * j:4 * j + 4, :, :].rearrange("p h s m -> p s h m") for j in range(NBLK)]
                   + [xT[:, :, j * BLK:(j + 1) * BLK] for j in range(NBLK)])

        def job_ap(j, part):
            d = job_dst[j][:, part]
            return d, (banks[j % 7][:, :].rearrange("p (h m) -> p h m", h=4) if NBLK <= j < 2 * NBLK else banks[j % 7][:, :])

        with nc.Block() as block:
            @block.sync
            def _(sp):
                sp.dma_start(ident[:, :], identity).then_inc(a["ident_in"], 16)
                sp.dma_start(ctx_tok.rearrange("p (i d) -> p i d", i=NT),
                             ctx.rearrange("b (i p) d -> p (b i) d", p=P)).then_inc(a["ctx_in"], 16)
                sp.dma_start(x_tok[:, :].rearrange("p (i d) -> p i d", i=NT),
                             x.rearrange("b (i p) d -> p (b i) d", p=P)).then_inc(a["x_in"], 16)
                for r in range(2):
                    sp.dma_start(raw_mk[:, :, r, :], mk[0].rearrange("m (h d) -> m h d", h=H)).then_inc(a["mk_in"], 16)
                sp.dma_start(mem_v[:, :], mv[0]).then_inc(a["mv_in"], 16)
                sp.dma_start(wo_sb[:, :, :], wo.rearrange("(j p) n -> p j n", p=P)).then_inc(a["wo_in"], 16)
                sp.dma_start(wd_sb[:, 0:NJE, :], w_down.rearrange("e f d -> (e f) d")
                             .rearrange("(j p) d -> p j d", p=P)).then_inc(a["wd_in"], 16)
                sp.dma_start(wd_sb[:, NJE:NJ - 1, :], sw_down[0:(NJ - 1 - NJE) * P, :]
                             .rearrange("(j p) d -> p j d", p=P)).then_inc(a["wd_in"], 16)
                sp.wait_ge(a["pad_done"], 1)
                sp.dma_start(wd_sb[0:LAST, NJ - 1, :], sw_down[(NJ - 1 - NJE) * P:FS, :]).then_inc(a["wd_in"], 16)
                sp.wait_ge(a["tr_done"], NBLK)
                sp.wait_ge(a["pad_done"], 2)
                for w, (we, ws) in enumerate(((w_gate, sw_gate), (w_up, sw_up))):
                    sp.dma_start(raw_gu[:, w, 0:FEX].rearrange("p (e f) -> p e f", e=E),
                                 we.rearrange("e d f -> d e f")).then_inc(a["gu_in"], 16)
                    sp.dma_start(raw_gu[:, w, FEX:FALL], ws).then_inc(a["gu_in"], 16)
                for s, n in (("mv_in", 1), ("wo_in", 1), ("wd_in", 3), ("gu_in", 4)):
                    sp.wait_ge(a[s], 16 * n)

            @block.scalar
            def _(act):
                act.dma_start(raw_w[:, 0, :], wq).then_inc(a["wq_in"], 16)
                act.dma_start(raw_w[:, 1, :], wk).then_inc(a["wk_in"], 16)
                act.dma_start(raw_w[:, 2, :], wv).then_inc(a["wv_in"], 16)
                for n, g in enumerate((g_xattn, g_ffn)):
                    act.dma_start(gains[:, n:n + 1], g.partition_broadcast(P)).then_inc(a["gain_in"], 16)
                for n, b in enumerate((wq_b, wk_b)):
                    for r in range(2):
                        act.dma_start(brows[:, n, r, :], b.rearrange("(h d) -> h d", h=H)).then_inc(a["bias_in"], 16)
                act.dma_start(gw_row[:, :], gate_w).then_inc(a["gate_in"], 16)
                act.dma_start(bv_bc[:, :], wv_b.partition_broadcast(P)).then_inc(a["bv_in"], 16)
                act.dma_start(bo_col[:, :], wo_b.rearrange("(p a) -> p a", a=1)).then_inc(a["bo_in"], 16)
                act.dma_start(raw_sel, selector).then_inc(a["misc_in"], 16)
                act.dma_start(iota_sb[:, :], iota).then_inc(a["misc_in"], 16)

                def high(j):
                    act.wait_ge(a["tr_done"], j + 1)
                    dst, src = job_ap(j, 0)
                    nc.scalar.activation(dst, src, ACT.Copy).then_inc(a["hi_done"], 1)

                def weight_high(w, sem):
                    act.wait_ge(a[("wq_in", "wk_in")[w]], 16)
                    for r in range(2):
                        nc.scalar.activation(wqk[:, w, 0, :, r, :], raw_w[:, w, :].rearrange("p (h d) -> p h d", h=H),
                                             ACT.Copy, scale=QSCALE if w == 0 else 1.0).then_inc(a[sem], 1)

                for j in range(NBLK):
                    high(j)
                act.wait_ge(a["var_ready"], 1)
                nc.scalar.activation(std[:, :], std[:, :], ACT.Sqrt).then_inc(a["std_ready"], 1)
                weight_high(0, "wq_hi")
                weight_high(1, "wk_hi")
                act.wait_ge(a["wv_in"], 16)
                nc.scalar.activation(wvs[:, 0, :], raw_w[:, 2, :], ACT.Copy).then_inc(a["wv_hi"], 1)
                for j in range(NBLK, NJOB):
                    high(j)
                act.wait_ge(a["small_done"], 1)
                nc.scalar.activation(bq8[:, :], banks[7][:, 0:H], ACT.Copy, scale=QSCALE).then_inc(a["small_copied"], 1)
                nc.scalar.activation(bk[:, :], banks[7][:, H:2 * H], ACT.Copy).then_inc(a["small_copied"], 1)
                nc.scalar.activation(gwT[:, 0, :], banks[7][:, 2 * H:2 * H + E], ACT.Copy).then_inc(a["gw_hi"], 1)
                act.wait_ge(a["gain_in"], 32)
                nc.scalar.activation(tg[:, :], gains[:, :], ACT.Tanh).then_inc(a["tanh_done"], 1)
                for s, n in (("bv_in", 16), ("bo_in", 16), ("misc_in", 32), ("tanh_done", 1), ("small_copied", 2)):
                    act.wait_ge(a[s], n)

            @block.gpsimd
            def _(pool):
                nc.gpsimd.memset(wd_sb[:, NJ - 1, :], 0.0).then_inc(a["pad_done"], 1)
                pool.wait_ge(a["tr_done"], NBLK)
                nc.gpsimd.memset(raw_gu[:, :, FALL:FPAD], 0.0).then_inc(a["pad_done"], 1)
                pool.wait_ge(a["ident_in"], 16)
                nc.gpsimd.tensor_copy(ident_b[:, :], ident[:, :]).then_inc(a["identb_done"], 1)
                pool.wait_ge(a["misc_in"], 32)
                nc.gpsimd.tensor_copy(sel_sb[:, :, :], raw_sel).then_inc(a["identb_done"], 1)
                pool.wait_ge(a["identb_done"], 2)
                pool.wait_ge(a["pad_done"], 2)

            @block.vector
            def _(dve):
                def low(j):
                    dve.wait_ge(a["hi_done"], j + 1)
                    hi, src = job_ap(j, 0)
                    lo, _ = job_ap(j, 1)
                    nc.vector.tensor_tensor(lo, src, hi.bitcast(F32), ALU.subtract).then_inc(a["lo_done"], 1)

                dve.wait_ge(a["x_in"], 16)
                for i in range(NT):
                    nc.vector.bn_stats(stat[:, i, :], x_tok[:, i * P:(i + 1) * P]).then_inc(a["ln_link"], 1)
                for i in range(NT):
                    dve.wait_ge(a["ln_link"], i + 1)
                    nc.vector.bn_aggr(mv_all[:, i, :], stat[:, i, :]).then_inc(a["ln_link"], 1)
                dve.wait_ge(a["ln_link"], 2 * NT)
                nc.vector.tensor_scalar(std[:, :], mv_all[:, :, 1], EPS, None, ALU.add).then_inc(a["var_ready"], 1)
                for j in range(NBLK):
                    low(j)
                dve.wait_ge(a["std_ready"], 1)
                nc.vector.reciprocal(rstd[:, :], std[:, :]).then_inc(a["ln_link"], 1)
                dve.wait_ge(a["ln_link"], 2 * NT + 1)
                for i in range(NT):
                    nc.vector.tensor_scalar(xln[:, i * P:(i + 1) * P], x_tok[:, i * P:(i + 1) * P], mv_all[:, i, 0:1],
                                            rstd[:, i:i + 1], ALU.subtract, ALU.mult).then_inc(a["ln_ready"], 1)
                for w, sem in enumerate(("wq_hi", "wk_hi")):
                    for r in range(2):
                        dve.wait_ge(a[sem], r + 1)
                        nc.vector.scalar_tensor_tensor(
                            wqk[:, w, 1, :, r, :], raw_w[:, w, :].rearrange("p (h d) -> p h d", h=H),
                            QSCALE if w == 0 else 1.0, wqk[:, w, 0, :, r, :].bitcast(F32),
                            ALU.mult, ALU.subtract).then_inc(a["w_lo"], 1)
                dve.wait_ge(a["wv_hi"], 1)
                nc.vector.tensor_tensor(wvs[:, 1, :], raw_w[:, 2, :], wvs[:, 0, :].bitcast(F32),
                                        ALU.subtract).then_inc(a["w_lo"], 1)
                for j in range(NBLK, NJOB):
                    low(j)
                dve.wait_ge(a["gw_hi"], 1)
                nc.vector.tensor_tensor(gwT[:, 1, :], banks[7][:, 2 * H:2 * H + E], gwT[:, 0, :].bitcast(F32),
                                        ALU.subtract).then_inc(a["gw_lo"], 1)
                dve.wait_ge(a["gw_lo"], 1)
                dve.wait_ge(a["w_lo"], 5)

            @block.tensor
            def _(pe):
                pe.wait_ge(a["ident_in"], 16)

                def transpose4(j, src, ready=None):
                    if j >= 7:
                        pe.wait_ge(a["lo_done"], j - 6)
                    for i in range(4):
                        if ready is not None:
                            pe.wait_ge(a[ready], 4 * (j - 2 * NBLK) + i + 1)
                        ins = nc.tensor.transpose(banks[j % 7][:, i * P:(i + 1) * P], src(i), ident[:, :])
                    ins.then_inc(a["tr_done"], 1)

                pe.wait_ge(a["ctx_in"], 16)
                for j in range(NBLK):
                    transpose4(j, lambda i: ctx_tok[:, (4 * j + i) * P:(4 * j + i + 1) * P])
                pe.wait_ge(a["mk_in"], 32)
                for j in range(NBLK):
                    transpose4(NBLK + j, lambda i: raw_mk[:, 4 * j + i, :, :].rearrange("p r d -> p (r d)"))
                pe.wait_ge(a["bias_in"], 64)
                pe.wait_ge(a["gate_in"], 16)
                for n in range(2):
                    nc.tensor.transpose(banks[7][:, n * H:(n + 1) * H], brows[:, n, :, :].rearrange("h r d -> h (r d)"),
                                        ident[0:H, 0:H])
                nc.tensor.transpose(banks[7][:, 2 * H:2 * H + E], gw_row[:, :], ident[0:E, 0:E]).then_inc(a["small_done"], 1)
                for j in range(NBLK):
                    transpose4(2 * NBLK + j, lambda i: xln[:, (4 * j + i) * P:(4 * j + i + 1) * P], ready="ln_ready")

        b = sems("ctx_blk q_proj k_proj q_hi q_lo k_hi k_lo mem0 mem1 v_proj v_ready scored maxed exped rsum_ready "
                 "normed transposed pT_act pT_dve weighed o_ready projected attn_sb attn_tr x1_done")
        mem_in = [b["mem0"], b["mem1"]]
        bank_q, bank_k = banks[0], banks[1]
        bank_s, bank_t = banks[2:4], banks[4:6]
        bank_o, bank_y = banks[6], banks[7]
        key_chunk = [[(0, 0), (0, 1), None], [None, (1, 0), (1, 1)]]

        with nc.Fori(0, NBLK) as blk:
            with nc.Block() as block:
                @block.sync
                def _(sp):
                    for h in range(H):
                        if h >= 2:
                            sp.wait_ge(b["scored"], CH * (h - 1))
                        sp.dma_start(k_st[:, h % 2, :, S:S + MEM].bitcast(F32), mem_k[:, h, :, :].bitcast(F32)).then_inc(mem_in[h % 2], 16)
                    for s in mem_in:
                        sp.wait_ge(s, 16 * H // 2)

                @block.tensor
                def _(pe):
                    def project(h, which):
                        bank = (bank_q, bank_k)[which]
                        src = (xT, cT)[which]
                        if h >= 1:
                            pe.wait_ge(b[("q_lo", "k_lo")[which]], h)
                            pe.wait_ge(b["v_ready"], 2 * ((h - 1) // GH + 1))
                        else:
                            pe.wait_ge(b["ctx_blk"], 1)
                            pe.wait_ge(b["v_ready"], 2)
                        for n, (ws, xs) in enumerate(((0, 0), (0, 1), (1, 0))):
                            ins = nc.tensor.matmul(bank[:, :], wqk[:, which, ws, h, :, :].rearrange("p r d -> p (r d)"),
                                                   src[:, xs, bass.ts(blk, BLK)], start=(n == 0), stop=(n == 2))
                        ins.then_inc(b[("q_proj", "k_proj")[which]], 1)

                    def values(g):
                        for half in range(2):
                            bank = (bank_q, bank_k)[half]
                            done = GH * g + 1
                            if g:
                                pe.wait_ge(b[("q_lo", "k_lo")[half]], done)
                            else:
                                pe.wait_ge(b["ctx_blk"], 1)
                            for c2 in range(2):
                                c = 2 * half + c2
                                for n, (cs, ws) in enumerate(((0, 0), (0, 1), (1, 0))):
                                    ins = nc.tensor.matmul(bank[:, c2 * GW:(c2 + 1) * GW], cT_blk[:, cs, c * P:(c + 1) * P],
                                                           wvs[:, ws, g * GW:(g + 1) * GW], start=(n == 0), stop=(n == 2))
                            ins.then_inc(b["v_proj"], 1)

                    def scores(h, c):
                        n = CH * h + c
                        if c == 0:
                            pe.wait_ge(b["q_lo"], h + 1)
                            pe.wait_ge(b["k_lo"], h + 1)
                            pe.wait_ge(mem_in[h % 2], 16 * (h // 2 + 1))
                        if n >= 2:
                            pe.wait_ge(b["exped"], n - 1)
                        at = S * (c // 2)
                        for part in range(2):
                            ins = nc.tensor.matmul(bank_s[n % 2][:, 0:T], q_st[:, h % 2, c * P:(c + 1) * P],
                                                   k_st[:, h % 2, part, at:at + T], start=(part == 0), stop=(part == 1))
                        ins.then_inc(b["scored"], 1)

                    def transpose(n):
                        pe.wait_ge(b["normed"], n + 1)
                        if n >= 2:
                            pe.wait_ge(b[("pT_act", "pT_dve")[n % 2]], n // 2)
                        for t in range(TC):
                            ins = nc.tensor.transpose(bank_t[n % 2][:, t * P:(t + 1) * P],
                                                      probs[:, n % PSLOT, t * P:(t + 1) * P], ident[:, :])
                        ins.then_inc(b["transposed"], 1)

                    def weigh(p, bb):
                        pe.wait_ge(b["pT_act"], 4 * (p + 1))
                        pe.wait_ge(b["pT_dve"], 4 * (p + 1))
                        if bb == 0 and p >= 1:
                            pe.wait_ge(b["o_ready"], p)
                        for t in range(TC):
                            for hh in range(2):
                                h = 2 * p + hh
                                where = key_chunk[bb][t]
                                if where is None:
                                    vals = mem_v[:, h * DK:(h + 1) * DK]
                                else:
                                    vals = v_sb[:, (h // GH) % 2, 2 * where[0] + where[1], (h % GH) * DK:(h % GH + 1) * DK]
                                ins = nc.tensor.matmul(bank_o[hh * DK:(hh + 1) * DK, bb * S:(bb + 1) * S], vals,
                                                       pT[:, h % 4, bb, t, :], start=(t == 0), stop=(t == TC - 1))
                        ins.then_inc(b["weighed"], 1)

                    def project_out(p):
                        pe.wait_ge(b["o_ready"], p + 1)
                        nc.tensor.matmul(bank_y[:, :], wo_sb[:, p, :], oT[:, p % 2, :], start=(p == 0),
                                         stop=(p == NPAIR - 1)).then_inc(b["projected"], 1)

                    values(0)
                    project(0, 0)
                    project(0, 1)
                    for h in range(H):
                        for c in range(CH):
                            scores(h, c)
                            if h >= 1:
                                transpose(CH * (h - 1) + c)
                            if c == 0 and h + 1 < H:
                                project(h + 1, 0)
                            if c == 1 and h + 1 < H:
                                project(h + 1, 1)
                            if c == 2 and h % GH == GH - 1 and h + 1 < H:
                                values((h + 1) // GH)
                            if h % 2 == 1 and h >= 3 and c in (1, 3):
                                weigh((h - 3) // 2, c // 2)
                            if h % 2 == 0 and h >= 4 and c == 1:
                                project_out((h - 4) // 2)
                    project_out(NPAIR - 2)
                    for c in range(CH):
                        transpose(CH * (H - 1) + c)
                    for bb in range(BB):
                        weigh(NPAIR - 1, bb)
                    project_out(NPAIR - 1)
                    pe.wait_ge(b["attn_sb"], 1)
                    for c in range(CH):
                        ins = nc.tensor.transpose(bank_o[:, c * P:(c + 1) * P], oT[:, 0, c * P:(c + 1) * P], ident[:, :])
                    ins.then_inc(b["attn_tr"], 1)

                @block.scalar
                def _(act):
                    def high(h, which):
                        act.wait_ge(b[("q_proj", "k_proj")[which]], h + 1)
                        if h >= 2:
                            act.wait_ge(b["scored"], CH * (h - 1))
                        if which == 0:
                            nc.scalar.activation(q_st[:, h % 2, :], bank_q[:, :], ACT.Identity,
                                                 bias=bq8[:, h:h + 1]).then_inc(b["q_hi"], 1)
                        else:
                            dst = k_st[:, h % 2, 0, :]
                            for bb in range(BB):
                                at = bb * (S + MEM)
                                nc.scalar.activation(dst[:, at:at + S], bank_k[:, bb * S:(bb + 1) * S], ACT.Identity,
                                                     bias=bk[:, h:h + 1]).then_inc(b["k_hi"], 1)

                    def exps(n):
                        act.wait_ge(b["maxed"], n + 1)
                        if n >= PSLOT:
                            act.wait_ge(b["transposed"], n - PSLOT + 1)
                        nc.scalar.activation(probs[:, n % PSLOT, :], bank_s[n % 2][:, 0:T], ACT.Exp,
                                             bias=nmax[:, n % PSLOT:n % PSLOT + 1],
                                             accum_out=psums[:, n % PSLOT:n % PSLOT + 1]).then_inc(b["exped"], 1)

                    def copy_out(n):
                        h, c = n // CH, n % CH
                        act.wait_ge(b["transposed"], n + 1)
                        if h >= 4:
                            act.wait_ge(b["weighed"], 2 * (h // 2 - 1))
                        nc.scalar.activation(pT[:, h % 4, c // 2, :, (c % 2) * P:(c % 2 + 1) * P],
                                             bank_t[0][:, 0:T].rearrange("p (t s) -> p t s", t=TC),
                                             ACT.Copy).then_inc(b["pT_act"], 1)

                    def pair_out(p):
                        act.wait_ge(b["weighed"], 2 * (p + 1))
                        if p >= 2:
                            act.wait_ge(b["projected"], p - 1)
                        nc.scalar.activation(oT[:, p % 2, :], bank_o[:, :], ACT.Copy).then_inc(b["o_ready"], 1)

                    high(0, 0)
                    high(0, 1)
                    for h in range(H):
                        for c in range(CH):
                            exps(CH * h + c)
                            if c % 2 == 0 and h >= 1:
                                copy_out(CH * (h - 1) + c)
                            if c == 1 and h + 1 < H:
                                high(h + 1, 0)
                            if c == 2 and h + 1 < H:
                                high(h + 1, 1)
                            if h % 2 == 0 and h >= 4 and c == 0:
                                pair_out((h - 4) // 2)
                    pair_out(NPAIR - 2)
                    for c in range(0, CH, 2):
                        copy_out(CH * (H - 1) + c)
                    pair_out(NPAIR - 1)
                    act.wait_ge(b["projected"], NPAIR)
                    nc.scalar.activation(oT[:, 0, :], bank_y[:, :], ACT.Identity, bias=bo_col[:, 0:1]).then_inc(b["attn_sb"], 1)

                @block.vector
                def _(dve):
                    def low(h, which):
                        if which == 0:
                            dve.wait_ge(b["q_hi"], h + 1)
                            lo = q_st[DK:P, h % 2, :]
                            nc.vector.scalar_tensor_tensor(lo, bank_q[DK:P, :], bq8[DK:P, h:h + 1], lo.bitcast(F32),
                                                           ALU.add, ALU.subtract).then_inc(b["q_lo"], 1)
                        else:
                            dve.wait_ge(b["k_hi"], 2 * (h + 1))
                            src = bank_k[:, :].rearrange("p (b s) -> p b s", b=BB)
                            hi, lo = (keys_of(h, part) for part in range(2))
                            nc.vector.scalar_tensor_tensor(lo, src, bk[:, h:h + 1], hi.bitcast(F32),
                                                           ALU.add, ALU.subtract).then_inc(b["k_lo"], 1)

                    def keys_of(h, part):
                        k = k_st[:, h % 2, part, :]
                        return bass.AP(k.tensor, k.offset, [list(k.ap[0]), [S + MEM, BB], [1, S]])

                    def maximum(n):
                        dve.wait_ge(b["scored"], n + 1)
                        nc.vector.tensor_reduce(nmax[:, n % PSLOT:n % PSLOT + 1], bank_s[n % 2][:, 0:T], axis=AX.X,
                                                op=ALU.max, negate=True).then_inc(b["maxed"], 1)

                    def inverse(n):
                        dve.wait_ge(b["exped"], n + 1)
                        nc.vector.reciprocal(rsum[:, n % PSLOT:n % PSLOT + 1],
                                             psums[:, n % PSLOT:n % PSLOT + 1]).then_inc(b["rsum_ready"], 1)

                    def copy_out(n):
                        h, c = n // CH, n % CH
                        dve.wait_ge(b["transposed"], n + 1)
                        if h >= 4:
                            dve.wait_ge(b["weighed"], 2 * (h // 2 - 1))
                        nc.vector.tensor_copy(pT[:, h % 4, c // 2, :, (c % 2) * P:(c % 2 + 1) * P],
                                              bank_t[1][:, 0:T].rearrange("p (t s) -> p t s", t=TC)).then_inc(b["pT_dve"], 1)

                    def values_out(g):
                        for half in range(2):
                            dve.wait_ge(b["v_proj"], 2 * g + half + 1)
                            if g >= 2:
                                dve.wait_ge(b["weighed"], 2 * (g - 1) * GH // 2)
                            bias = bv_bc[:, g * GW:(g + 1) * GW].unsqueeze(1).broadcast_to([P, 2, GW])
                            nc.vector.tensor_tensor(v_sb[:, g % 2, 2 * half:2 * half + 2, :],
                                                    (bank_q, bank_k)[half][:, :].rearrange("p (c n) -> p c n", c=2),
                                                    bias, ALU.add).then_inc(b["v_ready"], 1)

                    for part in range(1):
                        nc.vector.tensor_copy(cT_blk[:, :, :], cT[:, :, bass.ts(blk, BLK)].bitcast(F32)).then_inc(b["ctx_blk"], 1)
                    values_out(0)
                    low(0, 0)
                    low(0, 1)
                    for h in range(H):
                        for c in range(CH):
                            maximum(CH * h + c)
                            if CH * h + c >= 1:
                                inverse(CH * h + c - 1)
                            if c % 2 == 1 and h >= 1:
                                copy_out(CH * (h - 1) + c)
                            if c == 1 and h + 1 < H:
                                low(h + 1, 0)
                            if c == 2 and h + 1 < H:
                                low(h + 1, 1)
                            if c == 3 and h % GH == GH - 1 and h + 1 < H:
                                values_out((h + 1) // GH)
                    inverse(CH * H - 1)
                    for c in range(1, CH, 2):
                        copy_out(CH * (H - 1) + c)
                    dve.wait_ge(b["attn_tr"], 1)
                    xs = x_tok[:, bass.ts(blk, BLK)]
                    nc.vector.scalar_tensor_tensor(xs, bank_o[:, :], tg[:, 0:1], xs, ALU.mult, ALU.add).then_inc(b["x1_done"], 1)
                    dve.wait_ge(b["x1_done"], 1)

                @block.gpsimd
                def _(pool):
                    for n in range(CH * H):
                        pool.wait_ge(b["rsum_ready"], n + 1)
                        nc.gpsimd.tensor_tensor(probs[:, n % PSLOT, :], probs[:, n % PSLOT, :],
                                                rsum[:, n % PSLOT:n % PSLOT + 1].to_broadcast([P, T]),
                                                ALU.mult).then_inc(b["normed"], 1)

            nums = [s.num for s in b.values()]
            nc.gpsimd.sem_clear(range(min(nums), max(nums) + 1))
            nc.all_engine_barrier()

        c_ = sems("f_stat f_var f_std f_link f_ln f_tr f_hi f_lo r_log r_log_sb r_tr r_link r_exp r_exp_in r_parts r_parts_tr "
                  "r_cT gu_hi gu_lo r_zero")
        lg_row = stage[0:E, 0:TOK]
        lg = sb("lg", [P, NT, E])
        pr = sb("pr", [P, NT, E])
        m8 = sb("m8", [P, NT, E])
        i8 = sb("i8", [P, NT, E], U32)
        idf = sb("idf", [P, NT, TOPK])
        hit = sb("hit", [P, TOPK, NT, E])
        red = sb("red", [P, 4, NT])
        parts = probs[:, :, :].rearrange("p a b -> p (a b)")[:, 0:NT * P // 2].bitcast(BF16).rearrange("p (i k) -> p i k", i=NT)

        def part_ap(i):
            return parts[:, :, i * PART:i * PART + E]

        with nc.Block() as block:
            @block.vector
            def _(dve):
                for i in range(NT):
                    nc.vector.bn_stats(stat[:, i, :], x_tok[:, i * P:(i + 1) * P]).then_inc(c_["f_stat"], 1)
                for i in range(NT):
                    dve.wait_ge(c_["f_stat"], i + 1)
                    nc.vector.bn_aggr(mv_all[:, i, :], stat[:, i, :]).then_inc(c_["f_stat"], 1)
                dve.wait_ge(c_["f_stat"], 2 * NT)
                nc.vector.tensor_scalar(std[:, :], mv_all[:, :, 1], EPS, None, ALU.add).then_inc(c_["f_var"], 1)
                dve.wait_ge(c_["f_std"], 1)
                nc.vector.reciprocal(rstd[:, :], std[:, :]).then_inc(c_["f_link"], 1)
                dve.wait_ge(c_["f_link"], 1)
                for i in range(NT):
                    nc.vector.tensor_scalar(xln[:, i * P:(i + 1) * P], x_tok[:, i * P:(i + 1) * P], mv_all[:, i, 0:1],
                                            rstd[:, i:i + 1], ALU.subtract, ALU.mult).then_inc(c_["f_ln"], 1)
                for j in range(NBLK):
                    dve.wait_ge(c_["f_hi"], j + 1)
                    nc.vector.tensor_tensor(xT[:, 1, j * BLK:(j + 1) * BLK], banks[j][:, :],
                                            xT[:, 0, j * BLK:(j + 1) * BLK].bitcast(F32), ALU.subtract).then_inc(c_["f_lo"], 1)
                link = [0]

                def chain(ins):
                    link[0] += 1
                    ins.then_inc(c_["r_link"], 1)
                    dve.wait_ge(c_["r_link"], link[0])

                def over_e(v):
                    return v.unsqueeze(2).broadcast_to([P, NT, E])

                dve.wait_ge(c_["r_tr"], 1)
                logits = banks[6][:, 0:NT * E].rearrange("p (i e) -> p i e", i=NT)
                chain(nc.vector.tensor_reduce(red[:, 0, :], logits, axis=AX.X, op=ALU.max))
                nc.vector.tensor_tensor(lg[:, :, :], logits, over_e(red[:, 0, :]), ALU.subtract).then_inc(c_["r_exp_in"], 1)
                dve.wait_ge(c_["r_exp"], 1)
                chain(nc.vector.tensor_reduce(red[:, 1, :], pr[:, :, :], axis=AX.X, op=ALU.add))
                chain(nc.vector.reciprocal(red[:, 2, :], red[:, 1, :]))
                chain(nc.vector.tensor_tensor(pr[:, :, :], pr[:, :, :], over_e(red[:, 2, :]), ALU.mult))
                for i in range(NT):
                    ins = nc.vector.max(m8[:, i, :], pr[:, i, :])
                chain(ins)
                for i in range(NT):
                    ins = nc.vector.max_index(i8[:, i, :], m8[:, i, :], pr[:, i, :])
                chain(ins)
                chain(nc.vector.tensor_copy(idf[:, :, :], i8[:, :, 0:TOPK]))
                chain(nc.vector.tensor_tensor(red[:, 3, :], m8[:, :, 0], m8[:, :, 1], ALU.add))
                chain(nc.vector.tensor_scalar(red[:, 3, :], red[:, 3, :], 1e-20, None, ALU.add))
                chain(nc.vector.reciprocal(red[:, 0, :], red[:, 3, :]))
                for k in range(TOPK):
                    ins = nc.vector.tensor_tensor(hit[:, k, :, :], iota_sb[:, :].unsqueeze(1).broadcast_to([P, NT, E]),
                                                  over_e(idf[:, :, k]), ALU.is_equal)
                    chain(ins)
                chain(nc.vector.tensor_tensor(hit[:, 0, :, :], hit[:, 0, :, :], hit[:, 1, :, :], ALU.add))
                chain(nc.vector.tensor_tensor(pr[:, :, :], pr[:, :, :], over_e(red[:, 0, :]), ALU.mult))
                chain(nc.vector.scalar_tensor_tensor(pr[:, :, :], pr[:, :, :], ROUTE_SCALE, hit[:, 0, :, :], ALU.mult, ALU.mult))
                dve.wait_ge(c_["r_zero"], 1)
                chain(nc.vector.tensor_copy(part_ap(0), pr[:, :, :]))
                chain(nc.vector.tensor_tensor(pr[:, :, :], pr[:, :, :], part_ap(0), ALU.subtract))
                chain(nc.vector.tensor_copy(part_ap(1), pr[:, :, :]))
                chain(nc.vector.tensor_tensor(pr[:, :, :], pr[:, :, :], part_ap(1), ALU.subtract))
                chain(nc.vector.tensor_copy(part_ap(2), pr[:, :, :]))
                nc.vector.sem_inc(c_["r_parts"], 1)
                for w in range(2):
                    dve.wait_ge(c_["gu_hi"], w + 1)
                    nc.vector.tensor_tensor(gu_w[:, w, 1, :], raw_gu[:, w, :], gu_w[:, w, 0, :].bitcast(F32),
                                            ALU.subtract).then_inc(c_["gu_lo"], 1)
                for j in range(NBLK):
                    dve.wait_ge(c_["r_parts_tr"], j + 1)
                    nc.vector.tensor_copy(cT_route[:, j * BLK:(j + 1) * BLK],
                                          banks[j][:, 0:BLK // 2].bitcast(BF16)).then_inc(c_["r_cT"], 1)
                dve.wait_ge(c_["r_cT"], NBLK)
                dve.wait_ge(c_["gu_lo"], 2)

            @block.gpsimd
            def _(pool):
                nc.gpsimd.memset(parts, 0.0).then_inc(c_["r_zero"], 1)

            @block.scalar
            def _(act):
                act.wait_ge(c_["f_var"], 1)
                nc.scalar.activation(std[:, :], std[:, :], ACT.Sqrt).then_inc(c_["f_std"], 1)
                for w in range(2):
                    nc.scalar.activation(gu_w[:, w, 0, :], raw_gu[:, w, :], ACT.Copy).then_inc(c_["gu_hi"], 1)
                for j in range(NBLK):
                    act.wait_ge(c_["f_tr"], j + 1)
                    nc.scalar.activation(xT[:, 0, j * BLK:(j + 1) * BLK], banks[j][:, :], ACT.Copy).then_inc(c_["f_hi"], 1)
                for j in range(NBLK):
                    act.wait_ge(c_["r_log"], j + 1)
                    nc.scalar.activation(lg_row[:, j * BLK:(j + 1) * BLK], banks[4 + j % 2][0:E, :], ACT.Copy).then_inc(c_["r_log_sb"], 1)
                act.wait_ge(c_["r_exp_in"], 1)
                nc.scalar.activation(pr[:, :, :], lg[:, :, :], ACT.Exp).then_inc(c_["r_exp"], 1)

            @block.tensor
            def _(pe):
                for j in range(NBLK):
                    for i in range(4):
                        pe.wait_ge(c_["f_ln"], 4 * j + i + 1)
                        ins = nc.tensor.transpose(banks[j][:, i * P:(i + 1) * P],
                                                  xln[:, (4 * j + i) * P:(4 * j + i + 1) * P], ident[:, :])
                    ins.then_inc(c_["f_tr"], 1)
                for j in range(NBLK):
                    pe.wait_ge(c_["f_lo"], j + 1)
                    if j >= 2:
                        pe.wait_ge(c_["r_log_sb"], j - 1)
                    for n, (ws, xs) in enumerate(((0, 0), (0, 1), (1, 0))):
                        ins = nc.tensor.matmul(banks[4 + j % 2][0:E, :], gwT[:, ws, :], xT[:, xs, j * BLK:(j + 1) * BLK],
                                               start=(n == 0), stop=(n == 2))
                    ins.then_inc(c_["r_log"], 1)
                for i in range(NT):
                    pe.wait_ge(c_["r_log_sb"], i // 4 + 1)
                    ins = nc.tensor.transpose(banks[6][:, i * E:(i + 1) * E], lg_row[:, i * P:(i + 1) * P], ident[0:E, 0:E])
                ins.then_inc(c_["r_tr"], 1)
                pe.wait_ge(c_["r_parts"], 1)
                for j in range(NBLK):
                    for i in range(4):
                        ins = nc.tensor.transpose(banks[j][:, 0:BLK // 2].bitcast(BF16)[:, i * P:(i + 1) * P],
                                                  parts[:, 4 * j + i, :], ident_b[:, :])
                    ins.then_inc(c_["r_parts_tr"], 1)

        f = sems("gated upped routed silued hidden_up hidden down y_sb y_tr y_out stored")
        bank_g, bank_u, bank_c = banks[0:2], banks[2:4], banks[4:6]
        bank_d, bank_z = banks[6], banks[7]
        sil = ffn_work[:, 0:2 * BLK].rearrange("p (s t) -> p s t", s=2)
        hid = ffn_work[:, 2 * BLK:5 * BLK].rearrange("p (s t) -> p s t", s=3)
        yT = ffn_work[:, 5 * BLK:6 * BLK]
        res = ffn_work[:, 6 * BLK:7 * BLK]
        out_blk = out.rearrange("b s d -> (b s) d").rearrange("(n i p) d -> n p i d", n=NBLK, p=P)

        with nc.Fori(0, NBLK) as blk:
            with nc.Block() as block:
                @block.tensor
                def _(pe):
                    def up(j):
                        if j >= 2:
                            pe.wait_ge(f["silued"], j - 1)
                        for w, (bank, sem) in enumerate(((bank_g, "gated"), (bank_u, "upped"))):
                            if w == 1 and j >= 2:
                                pe.wait_ge(f["hidden_up"], j - 1)
                            for n, (ws, xs) in enumerate(((0, 0), (0, 1), (1, 0))):
                                ins = nc.tensor.matmul(bank[j % 2][:, :], gu_w[:, w, ws, j * P:(j + 1) * P],
                                                       xT[:, xs, bass.ts(blk, BLK)], start=(n == 0), stop=(n == 2))
                            ins.then_inc(f[sem], 1)
                        if j < NJE:
                            if j >= 2:
                                pe.wait_ge(f["hidden"], j - 1)
                            nc.tensor.matmul(bank_c[j % 2][:, :], sel_sb[:, j, :], cT_route[:, bass.ts(blk, BLK)],
                                             start=True, stop=True).then_inc(f["routed"], 1)

                    def down(j):
                        pe.wait_ge(f["hidden"], j + 1)
                        nc.tensor.matmul(bank_d[:, :], wd_sb[:, j, :], hid[:, j % 3, :], start=(j == 0),
                                         stop=(j == NJ - 1)).then_inc(f["down"], 1)

                    for j in range(NJ):
                        up(j)
                        if j >= 1:
                            down(j - 1)
                    down(NJ - 1)
                    pe.wait_ge(f["y_sb"], 1)
                    for c in range(CH):
                        ins = nc.tensor.transpose(bank_z[:, c * P:(c + 1) * P], yT[:, c * P:(c + 1) * P], ident[:, :])
                    ins.then_inc(f["y_tr"], 1)

                @block.scalar
                def _(act):
                    for j in range(NJ):
                        act.wait_ge(f["gated"], j + 1)
                        if j >= 2:
                            act.wait_ge(f["hidden_up"], j - 1)
                        nc.scalar.activation(sil[:, j % 2, :], bank_g[j % 2][:, :], ACT.Silu).then_inc(f["silued"], 1)
                    act.wait_ge(f["down"], NJ)
                    nc.scalar.activation(yT, bank_d[:, :], ACT.Copy).then_inc(f["y_sb"], 1)

                @block.vector
                def _(dve):
                    for j in range(NJ):
                        dve.wait_ge(f["silued"], j + 1)
                        dve.wait_ge(f["upped"], j + 1)
                        if j >= 3:
                            dve.wait_ge(f["down"], j - 2)
                        h = hid[:, j % 3, :]
                        ins = nc.vector.tensor_tensor(h, bank_u[j % 2][:, :], sil[:, j % 2, :], ALU.mult)
                        ins.then_inc(f["hidden_up"], 1)
                        if j < NJE:
                            dve.wait_ge(f["routed"], j + 1)
                            dve.wait_ge(f["hidden_up"], j + 1)
                            nc.vector.tensor_tensor(h, bank_c[j % 2][:, :], h, ALU.mult).then_inc(f["hidden"], 1)
                        else:
                            dve.wait_ge(f["hidden_up"], j + 1)
                            nc.vector.sem_inc(f["hidden"], 1)
                    dve.wait_ge(f["y_tr"], 1)
                    nc.vector.scalar_tensor_tensor(res, bank_z[:, :], tg[:, 1:2], x_tok[:, bass.ts(blk, BLK)],
                                                   ALU.mult, ALU.add).then_inc(f["y_out"], 1)

                @block.sync
                def _(sp):
                    sp.wait_ge(f["y_out"], 1)
                    sp.dma_start(out_blk[blk], res.rearrange("p (i d) -> p i d", i=CH)).then_inc(f["stored"], 16)
                    sp.wait_ge(f["stored"], 16)

            nums = [s.num for s in f.values()]
            nc.gpsimd.sem_clear(range(min(nums), max(nums) + 1))
            nc.all_engine_barrier()


_INS = ['x', 'ctx_1024', 'g_xattn', 'g_ffn', 'L0_xattn_wq_w', 'L0_xattn_wq_b', 'L0_xattn_wk_w', 'L0_xattn_wk_b',
        'L0_xattn_wv_w', 'L0_xattn_wv_b', 'L0_xattn_mk', 'L0_xattn_mv', 'L0_xattn_wo_w', 'L0_xattn_wo_b',
        'L0_ffn_gate_w', 'L0_ffn_w_gate', 'L0_ffn_w_up', 'L0_ffn_w_down', 'L0_ffn_sw_gate', 'L0_ffn_sw_up',
        'L0_ffn_sw_down']


def _constants():
    identity = np.eye(P, dtype=np.float32)
    selector = np.zeros((P, NJE, P), dtype=np.float32)
    expert = np.arange(FEX).reshape(NJE, P) // FE
    for part in range(3):
        for e in range(E):
            selector[part * PART + e] = expert == e
    iota = np.tile(np.arange(E, dtype=np.float32), (P, 1))
    return {"identity": identity, "selector": selector, "iota": iota}


def kernel(**inputs):
    import concourse.bacc as _bacc
    from concourse import mybir as _mybir
    from concourse.bass_utils import run_bass_kernel_spmd as _run

    nc = _bacc.Bacc("TRN2", target_bir_lowering=False, num_devices=1)
    arrays, args = {}, []
    named = [(n, np.ascontiguousarray(inputs[n])) for n in _INS] + list(_constants().items())
    for name, arr in named:
        arrays[f"in_{name}"] = arr
        args.append(nc.dram_tensor(f"in_{name}", arr.shape, _mybir.dt.from_np(arr.dtype), kind="ExternalInput").ap())
    out = nc.dram_tensor("out_0", (B, S, D), _mybir.dt.float32, kind="ExternalOutput").ap()
    flamingo_block(nc, *args, out)
    r = _run(nc, [arrays], core_ids=[0])
    return r.results[0]["out_0"]
```

```python
import numpy as np

import concourse.bass as bass
from concourse import mybir
from contextlib import ExitStack

F32 = mybir.dt.float32
F32R = mybir.dt.float32r
BF16 = mybir.dt.bfloat16
U32 = mybir.dt.uint32
ALU = mybir.AluOpType
ACT = mybir.ActivationFunctionType
AX = mybir.AxisListType

P = 128
B, S, D = 8, 256, 128
TOK = B * S
H, DK = 16, 64
HD = H * DK
MEM = 128
T = S + MEM
BLK = 512
NBLK = TOK // BLK
NT = TOK // P
CH = BLK // P
BB = BLK // S
TC = T // P
NPAIR = H // 2
GH = 4
GW = GH * DK
NG = H // GH
E, FE = 8, 176
FS = 352
FEX = E * FE
FALL = FEX + FS
NJ = -(-FALL // P)
FPAD = NJ * P
NJE = FEX // P
LAST = FALL - (NJ - 1) * P
TOPK = 2
ROUTE_SCALE = 2.5
EPS = 1e-5
QSCALE = DK ** -0.5
PSLOT = 8
SLOTS = 4
KW = S + MEM + S
KPART = 2 * (S + MEM)
KSLOT = KPART + KW
PART = 32

assert FEX % P == 0 and BB == 2 and TC == 3


SCHED = {
 "pe": {"Q": 0, "K": 0.3, "S0": 2, "S1": 2.25, "S2": 2.5, "S3": 2.75, "T0": 3.01, "T1": 3.26, "T2": 3.51, "T3": 3.76,
        "V0": 2.4, "V1": 2.9, "W0": 5.3, "W1": 5.8, "O": 6.3, "Z": 21.4},
 "act": {"Q": 0.2, "K": 0.5, "E0": 2.15, "E1": 2.4, "E2": 2.65, "E3": 2.9, "A0": 3.05, "A1": 3.55, "P": 6.0, "Y": 21.0},
 "dve": {"Q": 0.3, "K": 0.6, "M0": 2.1, "M1": 2.3, "M2": 2.6, "M3": 2.85, "I0": 2.36, "I1": 2.61, "I2": 2.86, "I3": 3.11,
         "D0": 3.3, "D1": 3.8, "V0": 2.5, "V1": 2.95, "B": 1.5, "X": 21.6},
}
RING, NTB = 4, 2


def turn(times):
    tasks = []
    for tok, w in times.items():
        kind = tok[0]
        for h in range(H):
            sub = int(tok[1]) if len(tok) > 1 else 0
            if kind in "STEMI":
                unit, per = CH * h + sub, CH * H
            elif kind in "AD":
                unit, per = 2 * h + sub, 2 * H
            elif kind in "QKPO":
                if h % 2: continue
                unit, per = h // 2, NPAIR
            elif kind == "W":
                if h % 2: continue
                unit, per = h + sub, 2 * NPAIR
            elif kind == "V":
                if h % GH: continue
                unit, per = 2 * (h // GH) + sub, 2 * NG
            else:
                if h: continue
                unit, per = 0, 1
            back = int((h + w) // H)
            assert back in (0, 1)
            tasks.append((h + w - H * back, kind, unit - per * back))
    return [(k, u) for _, k, u in sorted(tasks)]


def flamingo_block(nc, x, ctx, g_xattn, g_ffn, wq, wq_b, wk, wk_b, wv, wv_b, mk, mv, wo, wo_b,
                   gate_w, w_gate, w_up, w_down, sw_gate, sw_up, sw_down, identity, selector, iota, out):
    with ExitStack() as es:
        def sb(name, shape, dt=F32):
            return es.enter_context(nc.sbuf_tensor(name, shape, dt))

        def sems(names):
            return {n: es.enter_context(nc.semaphore(n)) for n in names.split()}

        x_pad = sb("x_pad", [P, BLK + TOK])
        x_tok = x_pad[:, BLK:BLK + TOK]
        xT = sb("xT", [P, 2, TOK], F32R)
        cT = sb("cT", [P, 2, TOK], F32R)
        cT_blk = sb("cT_blk", [P, 2, BLK], F32R)
        wqk = sb("wqk", [P, 2, 2, HD], F32R)
        wvs = sb("wvs", [P, 2, HD], F32R)
        mem_k = sb("mem_k", [P, H, 2, MEM], F32R)
        mem_v = sb("mem_v", [P, HD])
        k_st = sb("k_st", [P, SLOTS, KSLOT], F32R)
        q_st = sb("q_st", [P, SLOTS, BLK], F32R)
        qk_pair = sb("qk_pair", [P, 2, 2, BLK], F32R)
        v_sb = sb("v_sb", [P, 2, CH, GW])
        bv_bc = sb("bv_bc", [P, HD])
        wo_sb = sb("wo_sb", [P, NPAIR, D])
        probs = sb("probs", [P, PSLOT, T])
        pT = sb("pT", [P, 4, BB, TC, S])
        oT = sb("oT", [P, 2, BLK])
        ffn_work = sb("ffn_work", [P, 2 * FPAD])
        wd_sb = sb("wd_sb", [P, NJ, D])
        ident = sb("ident", [P, P])
        ident_b = sb("ident_b", [P, P], BF16)
        iota_sb = sb("iota_sb", [P, E])
        bq8 = sb("bq8", [P, NPAIR])
        bk = sb("bk", [P, NPAIR])
        gwT = sb("gwT", [P, 2, E], F32R)
        bo_col = sb("bo_col", [P, 1])
        gains = sb("gains", [P, 2])
        tg = sb("tg", [P, 2])
        stat = sb("stat", [P, NT, 6])
        mv_all = sb("mv_all", [P, NT, 2])
        std = sb("std", [P, NT])
        rstd = sb("rstd", [P, NT])
        nmax = sb("nmax", [P, PSLOT])
        psums = sb("psums", [P, PSLOT])
        rsum = sb("rsum", [P, PSLOT])

        gu_w = [v.rearrange("p (s f) -> p s f", s=2) for v in (cT[:, :, :].rearrange("p s t -> p (s t)")[:, 0:2 * FPAD],
                wqk[:, :, :, :].rearrange("p w s n -> p (w s n)")[:, 0:2 * FPAD])]
        stage = pT[:, :, :, :, :].rearrange("p a b c s -> p (a b c s)")
        raw_w = stage[:, 0:3 * HD].rearrange("p (w n) -> p w n", w=3)
        raw_mk = stage[:, 3 * HD:5 * HD].rearrange("p (h r d) -> p h r d", h=H, r=2)
        gw_row = stage[0:E, 5 * HD:5 * HD + D]
        brows = stage[0:NPAIR, 5 * HD + D:5 * HD + D + 2 * P].rearrange("j (n p) -> j n p", n=2)
        ctx_tok = ffn_work[:, 0:TOK]
        raw_gu = ffn_work[:, :].rearrange("p (w f) -> p w f", w=2)
        flat_probs = probs[:, :, :].rearrange("p a b -> p (a b)")
        cT_route = flat_probs[:, TOK // 2:TOK].bitcast(BF16)
        sel_sb = flat_probs[:, TOK:TOK + FEX // 2].bitcast(BF16).rearrange("p (j f) -> p j f", j=NJE)
        raw_sel = stage[:, TOK:TOK + FEX].rearrange("p (j f) -> p j f", j=NJE)
        xln = v_sb[:, :, :, :].rearrange("p a b c -> p (a b c)")

        banks = [es.enter_context(nc.psum_tensor(f"bank{i}", [P, 512], F32)) for i in range(8)]

        a = sems("cleared x_in ctx_in wq_in wk_in wv_in mk_in mv_in bias_in gate_in gain_in ident_in bv_in wo_in bo_in "
                 "misc_in gu_in wd_in pad_done var_ready std_ready ln_ready ln_link tr_done hi_done lo_done "
                 "small_done small_copied wq_hi wk_hi wv_hi w_lo tanh_done gu_raw_free identb_done gw_hi gw_lo")
        NJOB = 3 * NBLK
        job_dst = ([cT[:, :, j * BLK:(j + 1) * BLK] for j in range(NBLK)]
                   + [mem_k[:, 4 * j:4 * j + 4, :, :].rearrange("p h s m -> p s h m") for j in range(NBLK)]
                   + [xT[:, :, j * BLK:(j + 1) * BLK] for j in range(NBLK)])

        def job_ap(j, part):
            d = job_dst[j][:, part]
            return d, (banks[j % 7][:, :].rearrange("p (h m) -> p h m", h=4) if NBLK <= j < 2 * NBLK else banks[j % 7][:, :])

        with nc.Block() as block:
            @block.sync
            def _(sp):
                sp.dma_start(ident[:, :], identity).then_inc(a["ident_in"], 16)
                sp.dma_start(ctx_tok.rearrange("p (i d) -> p i d", i=NT),
                             ctx.rearrange("b (i p) d -> p (b i) d", p=P)).then_inc(a["ctx_in"], 16)
                sp.dma_start(x_tok[:, :].rearrange("p (i d) -> p i d", i=NT),
                             x.rearrange("b (i p) d -> p (b i) d", p=P)).then_inc(a["x_in"], 16)
                for r in range(2):
                    sp.dma_start(raw_mk[:, :, r, :], mk[0].rearrange("m (h d) -> m h d", h=H)).then_inc(a["mk_in"], 16)
                sp.dma_start(mem_v[:, :], mv[0]).then_inc(a["mv_in"], 16)
                sp.dma_start(wo_sb[:, :, :], wo.rearrange("(j p) n -> p j n", p=P)).then_inc(a["wo_in"], 16)
                sp.dma_start(wd_sb[:, 0:NJE, :], w_down.rearrange("e f d -> (e f) d")
                             .rearrange("(j p) d -> p j d", p=P)).then_inc(a["wd_in"], 16)
                sp.dma_start(wd_sb[:, NJE:NJ - 1, :], sw_down[0:(NJ - 1 - NJE) * P, :]
                             .rearrange("(j p) d -> p j d", p=P)).then_inc(a["wd_in"], 16)
                sp.wait_ge(a["pad_done"], 1)
                sp.dma_start(wd_sb[0:LAST, NJ - 1, :], sw_down[(NJ - 1 - NJE) * P:FS, :]).then_inc(a["wd_in"], 16)
                sp.wait_ge(a["tr_done"], NBLK)
                sp.wait_ge(a["pad_done"], 2)
                for w, (we, ws) in enumerate(((w_gate, sw_gate), (w_up, sw_up))):
                    sp.dma_start(raw_gu[:, w, 0:FEX].rearrange("p (e f) -> p e f", e=E),
                                 we.rearrange("e d f -> d e f")).then_inc(a["gu_in"], 16)
                    sp.dma_start(raw_gu[:, w, FEX:FALL], ws).then_inc(a["gu_in"], 16)
                for s, n in (("mv_in", 1), ("wo_in", 1), ("wd_in", 3), ("gu_in", 4)):
                    sp.wait_ge(a[s], 16 * n)

            @block.scalar
            def _(act):
                act.dma_start(raw_w[:, 0, :], wq).then_inc(a["wq_in"], 16)
                act.dma_start(raw_w[:, 1, :], wk).then_inc(a["wk_in"], 16)
                act.dma_start(raw_w[:, 2, :], wv).then_inc(a["wv_in"], 16)
                for n, g in enumerate((g_xattn, g_ffn)):
                    act.dma_start(gains[:, n:n + 1], g.partition_broadcast(P)).then_inc(a["gain_in"], 16)
                for n, b in enumerate((wq_b, wk_b)):
                    act.dma_start(brows[:, n, :], b.rearrange("(j p) -> j p", p=P)).then_inc(a["bias_in"], 16)
                act.dma_start(gw_row[:, :], gate_w).then_inc(a["gate_in"], 16)
                act.dma_start(bv_bc[:, :], wv_b.partition_broadcast(P)).then_inc(a["bv_in"], 16)
                act.dma_start(bo_col[:, :], wo_b.rearrange("(p a) -> p a", a=1)).then_inc(a["bo_in"], 16)
                act.dma_start(iota_sb[:, :], iota).then_inc(a["misc_in"], 16)

                def high(j):
                    act.wait_ge(a["tr_done"], j + 1)
                    dst, src = job_ap(j, 0)
                    nc.scalar.activation(dst, src, ACT.Copy).then_inc(a["hi_done"], 1)

                def weight_high(w, sem):
                    act.wait_ge(a[("wq_in", "wk_in")[w]], 16)
                    nc.scalar.activation(wqk[:, w, 0, :], raw_w[:, w, :], ACT.Copy,
                                         scale=QSCALE if w == 0 else 1.0).then_inc(a[sem], 1)

                for j in range(NBLK):
                    high(j)
                act.wait_ge(a["var_ready"], 1)
                nc.scalar.activation(std[:, :], std[:, :], ACT.Sqrt).then_inc(a["std_ready"], 1)
                weight_high(0, "wq_hi")
                weight_high(1, "wk_hi")
                act.wait_ge(a["wv_in"], 16)
                nc.scalar.activation(wvs[:, 0, :], raw_w[:, 2, :], ACT.Copy).then_inc(a["wv_hi"], 1)
                for j in range(NBLK, NJOB):
                    high(j)
                act.wait_ge(a["small_done"], 1)
                nc.scalar.activation(bq8[:, :], banks[7][:, 0:NPAIR], ACT.Copy, scale=QSCALE).then_inc(a["small_copied"], 1)
                nc.scalar.activation(bk[:, :], banks[7][:, NPAIR:2 * NPAIR], ACT.Copy).then_inc(a["small_copied"], 1)
                nc.scalar.activation(gwT[:, 0, :], banks[7][:, H:H + E], ACT.Copy).then_inc(a["gw_hi"], 1)
                act.wait_ge(a["gain_in"], 32)
                nc.scalar.activation(tg[:, :], gains[:, :], ACT.Tanh).then_inc(a["tanh_done"], 1)
                for s, n in (("bv_in", 16), ("bo_in", 16), ("misc_in", 16), ("tanh_done", 1), ("small_copied", 2)):
                    act.wait_ge(a[s], n)

            @block.gpsimd
            def _(pool):
                nc.gpsimd.memset(wd_sb[:, NJ - 1, :], 0.0).then_inc(a["pad_done"], 1)
                for t in (x_pad[:, 0:BLK], oT[:, :, :], nmax[:, :], q_st[:, 2:SLOTS, :].bitcast(F32), k_st[:, 2:SLOTS, :].bitcast(F32),
                          stage[:, 5 * HD + D + 2 * P:4 * BB * TC * S]):
                    nc.gpsimd.memset(t, 0.0).then_inc(a["cleared"], 1)
                for t in (psums[:, :], rsum[:, :]):
                    nc.gpsimd.memset(t, 1.0).then_inc(a["cleared"], 1)
                pool.wait_ge(a["cleared"], 8)
                pool.wait_ge(a["tr_done"], NBLK)
                nc.gpsimd.memset(raw_gu[:, :, FALL:FPAD], 0.0).then_inc(a["pad_done"], 1)
                pool.wait_ge(a["ident_in"], 16)
                nc.gpsimd.tensor_copy(ident_b[:, :], ident[:, :]).then_inc(a["identb_done"], 1)
                pool.wait_ge(a["identb_done"], 1)
                nc.gpsimd.memset(probs[:, :, :], 0.0).then_inc(a["cleared"], 1)
                pool.wait_ge(a["cleared"], 9)
                pool.wait_ge(a["pad_done"], 2)

            @block.vector
            def _(dve):
                def low(j):
                    dve.wait_ge(a["hi_done"], j + 1)
                    hi, src = job_ap(j, 0)
                    lo, _ = job_ap(j, 1)
                    nc.vector.tensor_tensor(lo, src, hi.bitcast(F32), ALU.subtract).then_inc(a["lo_done"], 1)

                dve.wait_ge(a["x_in"], 16)
                for i in range(NT):
                    nc.vector.bn_stats(stat[:, i, :], x_tok[:, i * P:(i + 1) * P]).then_inc(a["ln_link"], 1)
                for i in range(NT):
                    dve.wait_ge(a["ln_link"], i + 1)
                    nc.vector.bn_aggr(mv_all[:, i, :], stat[:, i, :]).then_inc(a["ln_link"], 1)
                dve.wait_ge(a["ln_link"], 2 * NT)
                nc.vector.tensor_scalar(std[:, :], mv_all[:, :, 1], EPS, None, ALU.add).then_inc(a["var_ready"], 1)
                for j in range(NBLK):
                    low(j)
                dve.wait_ge(a["std_ready"], 1)
                nc.vector.reciprocal(rstd[:, :], std[:, :]).then_inc(a["ln_link"], 1)
                dve.wait_ge(a["ln_link"], 2 * NT + 1)
                for i in range(NT):
                    nc.vector.tensor_scalar(xln[:, i * P:(i + 1) * P], x_tok[:, i * P:(i + 1) * P], mv_all[:, i, 0:1],
                                            rstd[:, i:i + 1], ALU.subtract, ALU.mult).then_inc(a["ln_ready"], 1)
                for w, sem in enumerate(("wq_hi", "wk_hi")):
                    dve.wait_ge(a[sem], 1)
                    nc.vector.scalar_tensor_tensor(wqk[:, w, 1, :], raw_w[:, w, :], QSCALE if w == 0 else 1.0,
                                                   wqk[:, w, 0, :].bitcast(F32), ALU.mult, ALU.subtract).then_inc(a["w_lo"], 1)
                dve.wait_ge(a["wv_hi"], 1)
                nc.vector.tensor_tensor(wvs[:, 1, :], raw_w[:, 2, :], wvs[:, 0, :].bitcast(F32),
                                        ALU.subtract).then_inc(a["w_lo"], 1)
                for j in range(NBLK, NJOB):
                    low(j)
                dve.wait_ge(a["gw_hi"], 1)
                nc.vector.tensor_tensor(gwT[:, 1, :], banks[7][:, H:H + E], gwT[:, 0, :].bitcast(F32),
                                        ALU.subtract).then_inc(a["gw_lo"], 1)
                dve.wait_ge(a["gw_lo"], 1)
                dve.wait_ge(a["w_lo"], 3)

            @block.tensor
            def _(pe):
                pe.wait_ge(a["ident_in"], 16)

                def transpose4(j, src, ready=None):
                    if j >= 7:
                        pe.wait_ge(a["lo_done"], j - 6)
                    for i in range(4):
                        if ready is not None:
                            pe.wait_ge(a[ready], 4 * (j - 2 * NBLK) + i + 1)
                        ins = nc.tensor.transpose(banks[j % 7][:, i * P:(i + 1) * P], src(i), ident[:, :])
                    ins.then_inc(a["tr_done"], 1)

                pe.wait_ge(a["ctx_in"], 16)
                for j in range(NBLK):
                    transpose4(j, lambda i: ctx_tok[:, (4 * j + i) * P:(4 * j + i + 1) * P])
                pe.wait_ge(a["mk_in"], 32)
                for j in range(NBLK):
                    transpose4(NBLK + j, lambda i: raw_mk[:, 4 * j + i, :, :].rearrange("p r d -> p (r d)"))
                pe.wait_ge(a["bias_in"], 32)
                pe.wait_ge(a["gate_in"], 16)
                for n in range(2):
                    nc.tensor.transpose(banks[7][:, n * NPAIR:(n + 1) * NPAIR], brows[:, n, :], ident[0:NPAIR, 0:NPAIR])
                nc.tensor.transpose(banks[7][:, H:H + E], gw_row[:, :], ident[0:E, 0:E]).then_inc(a["small_done"], 1)
                for j in range(NBLK):
                    transpose4(2 * NBLK + j, lambda i: xln[:, (4 * j + i) * P:(4 * j + i + 1) * P], ready="ln_ready")

        b = sems("ctx_blk q_proj k_proj q_hi q_lo k_hi k_lo slot0 slot1 slot2 slot3 v_proj v_ready scored maxed exped "
                 "rsum_ready normed transposed pT_act pT_dve weighed o_ready projected attn_sb attn_tr x1_done")
        slot_in = [f"slot{i}" for i in range(SLOTS)]
        SLOT_DMAS = 5
        TURN = dict(ctx_blk=1, q_proj=NPAIR, k_proj=NPAIR, q_hi=NPAIR, q_lo=NPAIR, k_hi=NPAIR, k_lo=NPAIR,
                    v_proj=2 * NG, v_ready=2 * NG, scored=CH * H, maxed=CH * H, exped=CH * H, rsum_ready=CH * H,
                    normed=CH * H, transposed=CH * H, pT_act=CH * H // 2, pT_dve=CH * H // 2, weighed=2 * NPAIR,
                    o_ready=NPAIR, projected=NPAIR, attn_sb=1, attn_tr=1, x1_done=1,
                    **{s: SLOT_DMAS * 16 * H // SLOTS for s in slot_in})
        ready = es.enter_context(nc.semaphore("ready"))
        ring, bank_t = banks[0:RING], banks[RING:RING + NTB]
        bank_o, bank_y = banks[6], banks[7]
        key_chunk = [[(0, 0), (0, 1), None], [None, (1, 0), (1, 1)]]
        FREED = {"Q": "q_lo", "K": "k_lo", "V": "v_ready", "S": "exped"}
        PER = {"Q": NPAIR, "K": NPAIR, "V": 2 * NG, "S": CH * H}
        pe_turn, act_turn, dve_turn = (turn(SCHED[e]) for e in ("pe", "act", "dve"))
        jobs = [(t, i) for t, i in pe_turn if t in PER]
        place = {(t, i % PER[t]): at % RING for at, (t, i) in enumerate(jobs)}
        assert len(jobs) % RING == 0 and len(jobs) == sum(PER.values())

        def bank_of(kind, i):
            return ring[place[kind, i % PER[kind]]]

        def late(tasks, kinds):
            return sum(t in kinds and i < 0 for t, i in tasks)

        MADE = dict(scored=(pe_turn, "S"), transposed=(pe_turn, "T"), weighed=(pe_turn, "W"), projected=(pe_turn, "O"),
                    attn_tr=(pe_turn, "Z"), maxed=(dve_turn, "M"), rsum_ready=(dve_turn, "I"), pT_dve=(dve_turn, "D"),
                    x1_done=(dve_turn, "X"), exped=(act_turn, "E"), pT_act=(act_turn, "A"), o_ready=(act_turn, "P"),
                    attn_sb=(act_turn, "Y"))
        assert not any(late(t, "QKVB") for t in (pe_turn, act_turn, dve_turn))

        def waiter(eng, blk):
            def done(name, i, each=1):
                eng.wait_ge(b[name], (blk + 1) * TURN[name] + (i + 1) * each)
            return done

        def turns(eng, tasks, do):
            with eng.Fori(0, NBLK) as blk:
                for t, i in tasks:
                    do(blk, waiter(eng, blk), t, i)
            for t, i in tasks:
                if i < 0:
                    do(NBLK, waiter(eng, NBLK), t, i)

        with nc.Block() as block:
            @block.sync
            def _(sp):
                for name in b:
                    if name in MADE:
                        start = TURN[name] - late(*MADE[name])
                    else:
                        start = TURN[name]
                    if start:
                        sp.sem_inc(b[name], start)
                sp.sem_inc(ready, 5)
                with sp.Fori(0, NBLK) as blk:
                    done = waiter(sp, blk)
                    for h in range(H):
                        p, hh = h // 2, h % 2
                        rows = slice(hh * DK, (hh + 1) * DK)
                        sem = b[slot_in[h % SLOTS]]
                        done("scored", CH * (h - SLOTS) + CH - 1)
                        k = k_st[:, h % SLOTS, S:S + MEM]
                        dst = bass.AP(k.tensor, k.offset, [list(k.ap[0]), [KPART, 2], [1, MEM]])
                        sp.dma_start(dst.bitcast(F32), mem_k[:, h, :, :].bitcast(F32)).then_inc(sem, 16)
                        done("q_lo", p)
                        for part in range(2):
                            sp.dma_start(q_st[part * DK:(part + 1) * DK, h % SLOTS, :].bitcast(F32),
                                         qk_pair[rows, 0, part, :].bitcast(F32)).then_inc(sem, 16)
                        done("k_lo", p)
                        for r in range(2):
                            k = k_st[r * DK:(r + 1) * DK, h % SLOTS, :]
                            dst = bass.AP(k.tensor, k.offset, [list(k.ap[0]), [S + MEM, 2 * BB], [1, S]]).bitcast(F32)
                            sp.dma_start(dst, qk_pair[rows, 1, :, :].bitcast(F32).rearrange("p s (b t) -> p (s b) t", b=BB)).then_inc(sem, 16)
                for s in slot_in:
                    sp.wait_ge(b[s], (NBLK + 1) * TURN[s])

            @block.tensor
            def _(pe):
                pe.wait_ge(ready, 5)
                nc.tensor.matmul(bank_y[:, :], oT[:, 0, 0:P], oT[:, 0, :], start=True, stop=False)

                def take(blk, done, kind, i):
                    at = jobs.index((kind, i)) - RING
                    while isinstance(blk, int) and at >= 0 and jobs[at][1] >= 0:
                        at -= RING
                    k, m = jobs[at]
                    done(FREED[k], m - (PER[k] if at < 0 else 0))
                    return bank_of(kind, i)

                def project(blk, done, which, p):
                    bank = take(blk, done, "QK"[which], p)
                    for n, (ws, xs) in enumerate(((0, 0), (0, 1), (1, 0))):
                        ins = nc.tensor.matmul(bank[:, :], wqk[:, which, ws, p * P:(p + 1) * P],
                                               (xT, cT)[which][:, xs, bass.ts(blk, BLK)], start=(n == 0), stop=(n == 2))
                    ins.then_inc(b[("q_proj", "k_proj")[which]], 1)

                def values(blk, done, i):
                    g, half = divmod(i, 2)
                    bank = take(blk, done, "V", i)
                    done("ctx_blk", 0)
                    for c2 in range(2):
                        c = 2 * half + c2
                        for n, (cs, ws) in enumerate(((0, 0), (0, 1), (1, 0))):
                            ins = nc.tensor.matmul(bank[:, c2 * GW:(c2 + 1) * GW], cT_blk[:, cs, c * P:(c + 1) * P],
                                                   wvs[:, ws, g * GW:(g + 1) * GW], start=(n == 0), stop=(n == 2))
                    ins.then_inc(b["v_proj"], 1)

                def scores(blk, done, n):
                    h, c = divmod(n, CH)
                    if c == 0:
                        done(slot_in[h % SLOTS], h // SLOTS, SLOT_DMAS * 16)
                    bank = take(blk, done, "S", n)
                    at = S * (c // 2)
                    for part in range(2):
                        ins = nc.tensor.matmul(bank[:, 0:T], q_st[:, h % SLOTS, c * P:(c + 1) * P],
                                               k_st[:, h % SLOTS, part * KPART + at:part * KPART + at + T], start=(part == 0), stop=(part == 1))
                    ins.then_inc(b["scored"], 1)

                def transpose(done, n):
                    done("normed", n)
                    done(("pT_act", "pT_dve")[n % 2], n // 2 - 1)
                    for t in range(TC):
                        ins = nc.tensor.transpose(bank_t[n % NTB][:, t * P:(t + 1) * P],
                                                  probs[:, n % PSLOT, t * P:(t + 1) * P], ident[:, :])
                    ins.then_inc(b["transposed"], 1)

                def weigh(done, i):
                    p, bb = divmod(i, 2)
                    done("pT_act", 4 * p + 3)
                    done("pT_dve", 4 * p + 3)
                    if bb == 0:
                        done("o_ready", p - 1)
                    for t in range(TC):
                        for hh in range(2):
                            h = (2 * p + hh) % H
                            where = key_chunk[bb][t]
                            if where is None:
                                vals = mem_v[:, h * DK:(h + 1) * DK]
                            else:
                                vals = v_sb[:, (h // GH) % 2, 2 * where[0] + where[1], (h % GH) * DK:(h % GH + 1) * DK]
                            ins = nc.tensor.matmul(bank_o[hh * DK:(hh + 1) * DK, bb * S:(bb + 1) * S], vals,
                                                   pT[:, h % 4, bb, t, :], start=(t == 0), stop=(t == TC - 1))
                    ins.then_inc(b["weighed"], 1)

                def project_out(done, p):
                    done("o_ready", p)
                    if p % NPAIR == 0:
                        done("x1_done", -1)
                    nc.tensor.matmul(bank_y[:, :], wo_sb[:, p % NPAIR, :], oT[:, p % 2, :], start=(p % NPAIR == 0),
                                     stop=(p % NPAIR == NPAIR - 1)).then_inc(b["projected"], 1)

                def turn_back(done, i):
                    done("attn_sb", i)
                    for c in range(CH):
                        ins = nc.tensor.transpose(bank_y[:, c * P:(c + 1) * P], oT[:, 0, c * P:(c + 1) * P], ident[:, :])
                    ins.then_inc(b["attn_tr"], 1)

                def do(blk, done, t, i):
                    if t == "S": scores(blk, done, i)
                    if t == "T": transpose(done, i)
                    if t == "Q": project(blk, done, 0, i)
                    if t == "K": project(blk, done, 1, i)
                    if t == "V": values(blk, done, i)
                    if t == "W": weigh(done, i)
                    if t == "O": project_out(done, i)
                    if t == "Z": turn_back(done, i)

                turns(pe, pe_turn, do)

            @block.scalar
            def _(act):
                act.wait_ge(ready, 5)

                def high(done, which, p):
                    done(("q_proj", "k_proj")[which], p)
                    for h in (2 * p - 2, 2 * p - 1):
                        done(slot_in[h % SLOTS], h // SLOTS, SLOT_DMAS * 16)
                    nc.scalar.activation(qk_pair[:, which, 0, :], bank_of("QK"[which], p)[:, :], ACT.Identity,
                                         bias=(bq8, bk)[which][:, p:p + 1]).then_inc(b[("q_hi", "k_hi")[which]], 1)

                def exps(done, n):
                    done("maxed", n)
                    done("transposed", n - PSLOT)
                    j = n % PSLOT
                    nc.scalar.activation(probs[:, j, :], bank_of("S", n)[:, 0:T], ACT.Exp, bias=nmax[:, j:j + 1],
                                         accum_out=psums[:, j:j + 1]).then_inc(b["exped"], 1)

                def copy_out(done, i):
                    n = 2 * i
                    h, c = divmod(n, CH)
                    done("transposed", n)
                    done("weighed", 2 * (h // 2 - 2) + 1)
                    nc.scalar.activation(pT[:, h % 4, c // 2, :, (c % 2) * P:(c % 2 + 1) * P],
                                         bank_t[0][:, 0:T].rearrange("p (t s) -> p t s", t=TC), ACT.Copy).then_inc(b["pT_act"], 1)

                def pair_out(done, p):
                    done("weighed", 2 * p + 1)
                    done("projected", p - 2)
                    if p % NPAIR == 0:
                        done("attn_tr", -1)
                    nc.scalar.activation(oT[:, p % 2, :], bank_o[:, :], ACT.Copy).then_inc(b["o_ready"], 1)

                def add_bias(done, i):
                    done("projected", (i + 1) * NPAIR - 1)
                    nc.scalar.activation(oT[:, 0, :], bank_y[:, :], ACT.Identity, bias=bo_col[:, 0:1]).then_inc(b["attn_sb"], 1)

                def do(blk, done, t, i):
                    if t == "E": exps(done, i)
                    if t == "A": copy_out(done, i)
                    if t == "Q": high(done, 0, i)
                    if t == "K": high(done, 1, i)
                    if t == "P": pair_out(done, i)
                    if t == "Y": add_bias(done, i)

                turns(act, act_turn, do)

            @block.vector
            def _(dve):
                dve.wait_ge(ready, 5)

                def low(done, which, p):
                    done(("q_hi", "k_hi")[which], p)
                    nc.vector.scalar_tensor_tensor(qk_pair[:, which, 1, :], bank_of("QK"[which], p)[:, :],
                                                   (bq8, bk)[which][:, p:p + 1], qk_pair[:, which, 0, :].bitcast(F32),
                                                   ALU.add, ALU.subtract).then_inc(b[("q_lo", "k_lo")[which]], 1)

                def maximum(done, n):
                    done("scored", n)
                    j = n % PSLOT
                    nc.vector.tensor_reduce(nmax[:, j:j + 1], bank_of("S", n)[:, 0:T], axis=AX.X, op=ALU.max,
                                            negate=True).then_inc(b["maxed"], 1)

                def inverse(done, n):
                    done("exped", n)
                    j = n % PSLOT
                    nc.vector.reciprocal(rsum[:, j:j + 1], psums[:, j:j + 1]).then_inc(b["rsum_ready"], 1)

                def copy_out(done, i):
                    n = 2 * i + 1
                    h, c = divmod(n, CH)
                    done("transposed", n)
                    done("weighed", 2 * (h // 2 - 2) + 1)
                    nc.vector.tensor_copy(pT[:, h % 4, c // 2, :, (c % 2) * P:(c % 2 + 1) * P],
                                          bank_t[1][:, 0:T].rearrange("p (t s) -> p t s", t=TC)).then_inc(b["pT_dve"], 1)

                def values_out(done, i):
                    g, half = divmod(i, 2)
                    done("v_proj", i)
                    done("weighed", 2 * (g - 1) * (GH // 2) - 1)
                    bias = bv_bc[:, g * GW:(g + 1) * GW].unsqueeze(1).broadcast_to([P, 2, GW])
                    nc.vector.tensor_tensor(v_sb[:, g % 2, 2 * half:2 * half + 2, :],
                                            bank_of("V", i)[:, :].rearrange("p (c n) -> p c n", c=2),
                                            bias, ALU.add).then_inc(b["v_ready"], 1)

                def fetch_ctx(blk, done, i):
                    done("v_proj", 2 * NG * i - 1)
                    nc.vector.tensor_copy(cT_blk[:, :, :], cT[:, :, bass.ts(blk, BLK)].bitcast(F32)).then_inc(b["ctx_blk"], 1)

                def residual(blk, done, i):
                    done("attn_tr", i)
                    xs = x_pad[:, bass.ts(blk, BLK)]
                    nc.vector.scalar_tensor_tensor(xs, bank_y[:, :], tg[:, 0:1], xs, ALU.mult, ALU.add).then_inc(b["x1_done"], 1)

                def do(blk, done, t, i):
                    if t == "M": maximum(done, i)
                    if t == "I": inverse(done, i)
                    if t == "D": copy_out(done, i)
                    if t == "Q": low(done, 0, i)
                    if t == "K": low(done, 1, i)
                    if t == "V": values_out(done, i)
                    if t == "B": fetch_ctx(blk, done, i)
                    if t == "X": residual(blk, done, i)

                turns(dve, dve_turn, do)
                dve.wait_ge(b["x1_done"], (NBLK + 1) * TURN["x1_done"])

            @block.gpsimd
            def _(pool):
                pool.wait_ge(ready, 5)
                with pool.Fori(0, NBLK) as blk:
                    done = waiter(pool, blk)
                    for n in range(CH * H):
                        done("rsum_ready", n)
                        j = n % PSLOT
                        nc.gpsimd.tensor_tensor(probs[:, j, :], probs[:, j, :], rsum[:, j:j + 1].to_broadcast([P, T]),
                                                ALU.mult).then_inc(b["normed"], 1)
        if SCHED.get("short"): return

        c_ = sems("f_stat f_var f_std f_link f_ln f_tr f_hi f_lo r_log r_log_sb r_tr r_link r_exp r_exp_in r_parts r_parts_tr "
                  "sel_in sel_done r_cT gu_hi gu_lo r_zero")
        lg_row = stage[0:E, 0:TOK]
        small = oT[:, :, :].rearrange("p a b -> p (a b)")
        lg, pr, m8, i8 = (small[:, k * NT * E:(k + 1) * NT * E].rearrange("p (i e) -> p i e", i=NT) for k in range(4))
        i8 = i8.bitcast(U32)
        hit = small[:, 4 * NT * E:6 * NT * E].rearrange("p (k i e) -> p k i e", k=TOPK, i=NT)
        idf = small[:, 6 * NT * E:6 * NT * E + NT * TOPK].rearrange("p (i k) -> p i k", i=NT)
        red = small[:, 6 * NT * E + NT * TOPK:6 * NT * E + NT * (TOPK + 4)].rearrange("p (k i) -> p k i", k=4)
        parts = probs[:, :, :].rearrange("p a b -> p (a b)")[:, 0:NT * P // 2].bitcast(BF16).rearrange("p (i k) -> p i k", i=NT)

        def part_ap(i):
            return parts[:, :, i * PART:i * PART + E]

        with nc.Block() as block:
            @block.vector
            def _(dve):
                for i in range(NT):
                    nc.vector.bn_stats(stat[:, i, :], x_tok[:, i * P:(i + 1) * P]).then_inc(c_["f_stat"], 1)
                for i in range(NT):
                    dve.wait_ge(c_["f_stat"], i + 1)
                    nc.vector.bn_aggr(mv_all[:, i, :], stat[:, i, :]).then_inc(c_["f_stat"], 1)
                dve.wait_ge(c_["f_stat"], 2 * NT)
                nc.vector.tensor_scalar(std[:, :], mv_all[:, :, 1], EPS, None, ALU.add).then_inc(c_["f_var"], 1)
                dve.wait_ge(c_["f_std"], 1)
                nc.vector.reciprocal(rstd[:, :], std[:, :]).then_inc(c_["f_link"], 1)
                dve.wait_ge(c_["f_link"], 1)
                for i in range(NT):
                    nc.vector.tensor_scalar(xln[:, i * P:(i + 1) * P], x_tok[:, i * P:(i + 1) * P], mv_all[:, i, 0:1],
                                            rstd[:, i:i + 1], ALU.subtract, ALU.mult).then_inc(c_["f_ln"], 1)
                for j in range(NBLK):
                    dve.wait_ge(c_["f_hi"], j + 1)
                    nc.vector.tensor_tensor(xT[:, 1, j * BLK:(j + 1) * BLK], banks[j][:, :],
                                            xT[:, 0, j * BLK:(j + 1) * BLK].bitcast(F32), ALU.subtract).then_inc(c_["f_lo"], 1)
                link = [0]

                def chain(ins):
                    link[0] += 1
                    ins.then_inc(c_["r_link"], 1)
                    dve.wait_ge(c_["r_link"], link[0])

                def over_e(v):
                    return v.unsqueeze(2).broadcast_to([P, NT, E])

                dve.wait_ge(c_["r_tr"], 1)
                logits = banks[6][:, 0:NT * E].rearrange("p (i e) -> p i e", i=NT)
                chain(nc.vector.tensor_reduce(red[:, 0, :], logits, axis=AX.X, op=ALU.max))
                nc.vector.tensor_tensor(lg[:, :, :], logits, over_e(red[:, 0, :]), ALU.subtract).then_inc(c_["r_exp_in"], 1)
                dve.wait_ge(c_["r_exp"], 1)
                chain(nc.vector.tensor_reduce(red[:, 1, :], pr[:, :, :], axis=AX.X, op=ALU.add))
                chain(nc.vector.reciprocal(red[:, 2, :], red[:, 1, :]))
                chain(nc.vector.tensor_tensor(pr[:, :, :], pr[:, :, :], over_e(red[:, 2, :]), ALU.mult))
                for i in range(NT):
                    ins = nc.vector.max(m8[:, i, :], pr[:, i, :])
                chain(ins)
                for i in range(NT):
                    ins = nc.vector.max_index(i8[:, i, :], m8[:, i, :], pr[:, i, :])
                chain(ins)
                chain(nc.vector.tensor_copy(idf[:, :, :], i8[:, :, 0:TOPK]))
                chain(nc.vector.tensor_tensor(red[:, 3, :], m8[:, :, 0], m8[:, :, 1], ALU.add))
                chain(nc.vector.tensor_scalar(red[:, 3, :], red[:, 3, :], 1e-20, None, ALU.add))
                chain(nc.vector.reciprocal(red[:, 0, :], red[:, 3, :]))
                for k in range(TOPK):
                    ins = nc.vector.tensor_tensor(hit[:, k, :, :], iota_sb[:, :].unsqueeze(1).broadcast_to([P, NT, E]),
                                                  over_e(idf[:, :, k]), ALU.is_equal)
                    chain(ins)
                chain(nc.vector.tensor_tensor(hit[:, 0, :, :], hit[:, 0, :, :], hit[:, 1, :, :], ALU.add))
                chain(nc.vector.tensor_tensor(pr[:, :, :], pr[:, :, :], over_e(red[:, 0, :]), ALU.mult))
                chain(nc.vector.scalar_tensor_tensor(pr[:, :, :], pr[:, :, :], ROUTE_SCALE, hit[:, 0, :, :], ALU.mult, ALU.mult))
                dve.wait_ge(c_["r_zero"], 1)
                chain(nc.vector.tensor_copy(part_ap(0), pr[:, :, :]))
                chain(nc.vector.tensor_tensor(pr[:, :, :], pr[:, :, :], part_ap(0), ALU.subtract))
                chain(nc.vector.tensor_copy(part_ap(1), pr[:, :, :]))
                chain(nc.vector.tensor_tensor(pr[:, :, :], pr[:, :, :], part_ap(1), ALU.subtract))
                chain(nc.vector.tensor_copy(part_ap(2), pr[:, :, :]))
                nc.vector.sem_inc(c_["r_parts"], 1)
                for w in range(2):
                    dve.wait_ge(c_["gu_hi"], w + 1)
                    nc.vector.tensor_tensor(gu_w[w][:, 1, :], raw_gu[:, w, :], gu_w[w][:, 0, :].bitcast(F32),
                                            ALU.subtract).then_inc(c_["gu_lo"], 1)
                for j in range(NBLK):
                    dve.wait_ge(c_["r_parts_tr"], j + 1)
                    nc.vector.tensor_copy(cT_route[:, j * BLK:(j + 1) * BLK],
                                          banks[j][:, 0:BLK // 2].bitcast(BF16)).then_inc(c_["r_cT"], 1)
                dve.wait_ge(c_["r_cT"], NBLK)
                dve.wait_ge(c_["gu_lo"], 2)

            @block.sync
            def _(sp):
                sp.dma_start(raw_sel, selector).then_inc(c_["sel_in"], 16)

            @block.gpsimd
            def _(pool):
                nc.gpsimd.memset(parts, 0.0).then_inc(c_["r_zero"], 1)
                pool.wait_ge(c_["sel_in"], 16)
                nc.gpsimd.tensor_copy(sel_sb, raw_sel).then_inc(c_["sel_done"], 1)
                pool.wait_ge(c_["sel_done"], 1)

            @block.scalar
            def _(act):
                act.wait_ge(c_["f_var"], 1)
                nc.scalar.activation(std[:, :], std[:, :], ACT.Sqrt).then_inc(c_["f_std"], 1)
                for w in range(2):
                    nc.scalar.activation(gu_w[w][:, 0, :], raw_gu[:, w, :], ACT.Copy).then_inc(c_["gu_hi"], 1)
                for j in range(NBLK):
                    act.wait_ge(c_["f_tr"], j + 1)
                    nc.scalar.activation(xT[:, 0, j * BLK:(j + 1) * BLK], banks[j][:, :], ACT.Copy).then_inc(c_["f_hi"], 1)
                for j in range(NBLK):
                    act.wait_ge(c_["r_log"], j + 1)
                    nc.scalar.activation(lg_row[:, j * BLK:(j + 1) * BLK], banks[4 + j % 2][0:E, :], ACT.Copy).then_inc(c_["r_log_sb"], 1)
                act.wait_ge(c_["r_exp_in"], 1)
                nc.scalar.activation(pr[:, :, :], lg[:, :, :], ACT.Exp).then_inc(c_["r_exp"], 1)

            @block.tensor
            def _(pe):
                for j in range(NBLK):
                    for i in range(4):
                        pe.wait_ge(c_["f_ln"], 4 * j + i + 1)
                        ins = nc.tensor.transpose(banks[j][:, i * P:(i + 1) * P],
                                                  xln[:, (4 * j + i) * P:(4 * j + i + 1) * P], ident[:, :])
                    ins.then_inc(c_["f_tr"], 1)
                for j in range(NBLK):
                    pe.wait_ge(c_["f_lo"], j + 1)
                    if j >= 2:
                        pe.wait_ge(c_["r_log_sb"], j - 1)
                    for n, (ws, xs) in enumerate(((0, 0), (0, 1), (1, 0))):
                        ins = nc.tensor.matmul(banks[4 + j % 2][0:E, :], gwT[:, ws, :], xT[:, xs, j * BLK:(j + 1) * BLK],
                                               start=(n == 0), stop=(n == 2))
                    ins.then_inc(c_["r_log"], 1)
                for i in range(NT):
                    pe.wait_ge(c_["r_log_sb"], i // 4 + 1)
                    ins = nc.tensor.transpose(banks[6][:, i * E:(i + 1) * E], lg_row[:, i * P:(i + 1) * P], ident[0:E, 0:E])
                ins.then_inc(c_["r_tr"], 1)
                pe.wait_ge(c_["r_parts"], 1)
                for j in range(NBLK):
                    for i in range(4):
                        ins = nc.tensor.transpose(banks[j][:, 0:BLK // 2].bitcast(BF16)[:, i * P:(i + 1) * P],
                                                  parts[:, 4 * j + i, :], ident_b[:, :])
                    ins.then_inc(c_["r_parts_tr"], 1)

        f = sems("gated upped routed silued hidden_up hidden down y_sb y_tr y_out stored")
        bank_g, bank_u, bank_c = banks[0:2], banks[2:4], banks[4:6]
        bank_d, bank_z = banks[6], banks[7]
        sil = ffn_work[:, 0:2 * BLK].rearrange("p (s t) -> p s t", s=2)
        hid = ffn_work[:, 2 * BLK:5 * BLK].rearrange("p (s t) -> p s t", s=3)
        yT = ffn_work[:, 5 * BLK:6 * BLK]
        res = ffn_work[:, 6 * BLK:7 * BLK]
        out_blk = out.rearrange("b s d -> (b s) d").rearrange("(n i p) d -> n p i d", n=NBLK, p=P)

        with nc.Fori(0, NBLK) as blk:
            with nc.Block() as block:
                @block.tensor
                def _(pe):
                    def up(j):
                        if j >= 2:
                            pe.wait_ge(f["silued"], j - 1)
                        for w, (bank, sem) in enumerate(((bank_g, "gated"), (bank_u, "upped"))):
                            if w == 1 and j >= 2:
                                pe.wait_ge(f["hidden_up"], j - 1)
                            for n, (ws, xs) in enumerate(((0, 0), (0, 1), (1, 0))):
                                ins = nc.tensor.matmul(bank[j % 2][:, :], gu_w[w][:, ws, j * P:(j + 1) * P],
                                                       xT[:, xs, bass.ts(blk, BLK)], start=(n == 0), stop=(n == 2))
                            ins.then_inc(f[sem], 1)
                        if j < NJE:
                            if j >= 2:
                                pe.wait_ge(f["hidden"], j - 1)
                            nc.tensor.matmul(bank_c[j % 2][:, :], sel_sb[:, j, :], cT_route[:, bass.ts(blk, BLK)],
                                             start=True, stop=True).then_inc(f["routed"], 1)

                    def down(j):
                        pe.wait_ge(f["hidden"], j + 1)
                        nc.tensor.matmul(bank_d[:, :], wd_sb[:, j, :], hid[:, j % 3, :], start=(j == 0),
                                         stop=(j == NJ - 1)).then_inc(f["down"], 1)

                    for j in range(NJ):
                        up(j)
                        if j >= 1:
                            down(j - 1)
                    down(NJ - 1)
                    pe.wait_ge(f["y_sb"], 1)
                    for c in range(CH):
                        ins = nc.tensor.transpose(bank_z[:, c * P:(c + 1) * P], yT[:, c * P:(c + 1) * P], ident[:, :])
                    ins.then_inc(f["y_tr"], 1)

                @block.scalar
                def _(act):
                    for j in range(NJ):
                        act.wait_ge(f["gated"], j + 1)
                        if j >= 2:
                            act.wait_ge(f["hidden_up"], j - 1)
                        nc.scalar.activation(sil[:, j % 2, :], bank_g[j % 2][:, :], ACT.Silu).then_inc(f["silued"], 1)
                    act.wait_ge(f["down"], NJ)
                    nc.scalar.activation(yT, bank_d[:, :], ACT.Copy).then_inc(f["y_sb"], 1)

                @block.vector
                def _(dve):
                    for j in range(NJ):
                        dve.wait_ge(f["silued"], j + 1)
                        dve.wait_ge(f["upped"], j + 1)
                        if j >= 3:
                            dve.wait_ge(f["down"], j - 2)
                        h = hid[:, j % 3, :]
                        ins = nc.vector.tensor_tensor(h, bank_u[j % 2][:, :], sil[:, j % 2, :], ALU.mult)
                        ins.then_inc(f["hidden_up"], 1)
                        if j < NJE:
                            dve.wait_ge(f["routed"], j + 1)
                            dve.wait_ge(f["hidden_up"], j + 1)
                            nc.vector.tensor_tensor(h, bank_c[j % 2][:, :], h, ALU.mult).then_inc(f["hidden"], 1)
                        else:
                            dve.wait_ge(f["hidden_up"], j + 1)
                            nc.vector.sem_inc(f["hidden"], 1)
                    dve.wait_ge(f["y_tr"], 1)
                    nc.vector.scalar_tensor_tensor(res, bank_z[:, :], tg[:, 1:2], x_tok[:, bass.ts(blk, BLK)],
                                                   ALU.mult, ALU.add).then_inc(f["y_out"], 1)

                @block.sync
                def _(sp):
                    sp.wait_ge(f["y_out"], 1)
                    sp.dma_start(out_blk[blk], res.rearrange("p (i d) -> p i d", i=CH)).then_inc(f["stored"], 16)
                    sp.wait_ge(f["stored"], 16)

            nums = [s.num for s in f.values()]
            nc.gpsimd.sem_clear(range(min(nums), max(nums) + 1))
            nc.all_engine_barrier()


_INS = ['x', 'ctx_1024', 'g_xattn', 'g_ffn', 'L0_xattn_wq_w', 'L0_xattn_wq_b', 'L0_xattn_wk_w', 'L0_xattn_wk_b',
        'L0_xattn_wv_w', 'L0_xattn_wv_b', 'L0_xattn_mk', 'L0_xattn_mv', 'L0_xattn_wo_w', 'L0_xattn_wo_b',
        'L0_ffn_gate_w', 'L0_ffn_w_gate', 'L0_ffn_w_up', 'L0_ffn_w_down', 'L0_ffn_sw_gate', 'L0_ffn_sw_up',
        'L0_ffn_sw_down']


def _constants():
    identity = np.eye(P, dtype=np.float32)
    selector = np.zeros((P, NJE, P), dtype=np.float32)
    expert = np.arange(FEX).reshape(NJE, P) // FE
    for part in range(3):
        for e in range(E):
            selector[part * PART + e] = expert == e
    iota = np.tile(np.arange(E, dtype=np.float32), (P, 1))
    return {"identity": identity, "selector": selector, "iota": iota}


def kernel(**inputs):
    import concourse.bacc as _bacc
    from concourse import mybir as _mybir
    from concourse.bass_utils import run_bass_kernel_spmd as _run

    nc = _bacc.Bacc("TRN2", target_bir_lowering=False, num_devices=1)
    arrays, args = {}, []
    named = [(n, np.ascontiguousarray(inputs[n])) for n in _INS] + list(_constants().items())
    for name, arr in named:
        arrays[f"in_{name}"] = arr
        args.append(nc.dram_tensor(f"in_{name}", arr.shape, _mybir.dt.from_np(arr.dtype), kind="ExternalInput").ap())
    out = nc.dram_tensor("out_0", (B, S, D), _mybir.dt.float32, kind="ExternalOutput").ap()
    flamingo_block(nc, *args, out)
    r = _run(nc, [arrays], core_ids=[0])
    return r.results[0]["out_0"]
```

```python
import numpy as np

import concourse.bass as bass
from concourse import mybir
from contextlib import ExitStack

F32 = mybir.dt.float32
F32R = mybir.dt.float32r
BF16 = mybir.dt.bfloat16
U32 = mybir.dt.uint32
ALU = mybir.AluOpType
ACT = mybir.ActivationFunctionType
AX = mybir.AxisListType

P = 128
B, S, D = 8, 256, 128
TOK = B * S
H, DK = 16, 64
HD = H * DK
MEM = 128
T = S + MEM
BLK = 512
NBLK = TOK // BLK
NT = TOK // P
CH = BLK // P
BB = BLK // S
TC = T // P
NPAIR = H // 2
GH = 4
GW = GH * DK
NG = H // GH
E, FE = 8, 176
FS = 352
FEX = E * FE
FALL = FEX + FS
NJ = -(-FALL // P)
FPAD = NJ * P
NJE = FEX // P
NSH = NJ - NJE
LAST = FALL - (NJ - 1) * P
TOPK = 2
ROUTE_SCALE = 2.5
EPS = 1e-5
QSCALE = DK ** -0.5
PSLOT = 8
SLOTS = 4
KW = S + MEM + S
KPART = 2 * (S + MEM)
KSLOT = KPART + KW
PART = 32

assert FEX % P == 0 and BB == 2 and TC == 3


SCHED = {
 "pe": {"Q": 0.042, "K": 0.141, "S0": 1.748, "S1": 2.107, "S2": 2.554, "S3": 2.721, "T0": 2.965, "T1": 3.345,
    "T2": 3.61, "T3": 3.733, "V0": 2.324, "V1": 3.471, "W0": 5.272, "W1": 5.91, "O": 6.394, "Z": 21.072,
    "L0": 22.978, "L1": 22.693, "G": 23.731},
 "act": {"Q": 0.153, "K": 0.196, "E0": 2.09, "E1": 2.29, "E2": 2.765, "E3": 2.919, "A0": 3.171, "A1": 3.323,
    "P": 5.924, "Y": 20.464, "L0": 22.528, "L1": 22.848, "X": 23.352, "A2": 3.207},
 "dve": {"Q": 0.277, "K": 0.595, "M0": 2.083, "M1": 2.192, "M2": 2.653, "M3": 2.958, "I0": 2.58, "I1": 2.913,
    "I2": 3.157, "I3": 3.135, "V0": 2.646, "V1": 3.475, "B": 2.151, "X": 21.16, "R": 21.61, "N": 21.83,
    "G": 21.96, "F": 22.167, "U": 22.399, "L0": 22.859, "L1": 23.103, "P": 6.181, "H0": 23.795, "H1": 24.135,
    "H2": 24.439, "H3": 25.574, "D": 3.918},
 "pool": {"C0": 1.857, "C1": 2.457, "C2": 2.045, "C3": 2.827, "R": 21.419},
}
RING, NTB = 4, 2


def turn(times):
    due, tasks = {}, []
    for tok, w in times.items():
        kind = tok[0]
        for h in range(H):
            sub = int(tok[1]) if len(tok) > 1 else 0
            if kind in "STEMIC":
                unit, per = CH * h + sub, CH * H
            elif kind == "A":
                unit, per = (CH - 1) * h + sub, (CH - 1) * H
            elif kind == "D":
                unit, per = h, H
            elif kind in "QKPO":
                if h % 2: continue
                unit, per = h // 2, NPAIR
            elif kind == "W":
                if h % 2: continue
                unit, per = h + sub, 2 * NPAIR
            elif kind == "L":
                if h: continue
                unit, per = sub, 2
            elif kind == "H":
                if h: continue
                unit, per = sub, 4
            elif kind == "V":
                if h % GH: continue
                unit, per = 2 * (h // GH) + sub, 2 * NG
            else:
                if h: continue
                unit, per = 0, 1
            due.setdefault(kind, []).append((h + w, unit, per))
    for kind, d in due.items():
        when = sorted(t for t, _, _ in d)
        assert when[-1] - H < when[0]
        for t, (unit, per) in zip(when, sorted((u, per) for _, u, per in d)):
            back = int(t // H)
            assert back in (0, 1)
            tasks.append((t - H * back, kind, unit - per * back))
    return [(k, u) for _, k, u in sorted(tasks)]


FSCHED = {
 "pe": {"G": 0.224, "P": 2.38, "R": 3.843, "U": 0.407, "D": 4.481, "Z": 18.411},
 "act": {"L": 0.885, "A": 2.113, "Y": 17.815},
 "dve": {"F": 1.765, "C": 2.562, "H": 0.82, "N": 3.848, "X": 18.226},
 "pool": {"B": 4.651},
}


def fturn(times):
    tasks = []
    for kind, w in times.items():
        units = NJE if kind in "RN" else 1 if kind in "YZXFPC" else NJ
        for u in range(units):
            back = int((u + w) // NJ)
            assert back in (0, 1)
            tasks.append((u + w - NJ * back, kind, u - units * back))
    return [(k, u) for _, k, u in sorted(tasks)]


def flamingo_block(nc, x, ctx, g_xattn, g_ffn, wq, wq_b, wk, wk_b, wv, wv_b, mk, mv, wo, wo_b,
                   gate_w, w_gate, w_up, w_down, sw_gate, sw_up, sw_down, identity, selector, iota, out):
    with ExitStack() as es:
        def sb(name, shape, dt=F32):
            return es.enter_context(nc.sbuf_tensor(name, shape, dt))

        def sems(names):
            return {n: es.enter_context(nc.semaphore(n)) for n in names.split()}

        x_pad = sb("x_pad", [P, BLK + TOK])
        x_tok = x_pad[:, BLK:BLK + TOK]
        xT_pad = sb("xT_pad", [P, 2, BLK + TOK], F32R)
        xT = xT_pad[:, :, BLK:BLK + TOK]
        x2ln = sb("x2ln", [P, BLK])
        comb_pad = sb("comb_pad", [P, (NBLK + 1) * CH * E])
        route_work = sb("route_work", [P, 4 * CH * E + CH * TOPK + 4 * CH])
        cT = sb("cT", [P, 2, TOK], F32R)
        cT_blk = sb("cT_blk", [P, 2, BLK], F32R)
        wqk = sb("wqk", [P, 2, 2, HD], F32R)
        wvs = sb("wvs", [P, 2, HD], F32R)
        mem_k = sb("mem_k", [P, NPAIR, 2, MEM], F32R)
        mem_v = sb("mem_v", [P, HD])
        k_st = sb("k_st", [P, SLOTS, KSLOT], F32R)
        q_st = sb("q_st", [P, SLOTS, BLK], F32R)
        qk_pair = sb("qk_pair", [P, 2, 2, BLK], F32R)
        v_sb = sb("v_sb", [P, 2, CH, GW])
        bv_bc = sb("bv_bc", [P, HD])
        wo_sb = sb("wo_sb", [P, 2, NPAIR, D], F32R)
        probs = sb("probs", [P, PSLOT, T])
        pT = sb("pT", [P, 4, BB, TC, S])
        oT = sb("oT", [P, 2, 2, BLK], F32R)
        ffn_work = sb("ffn_work", [P, 2 * FPAD])
        ident = sb("ident", [P, P])
        ident_b = sb("ident_b", [P, P], BF16)
        iota_sb = sb("iota_sb", [P, E])
        bq8 = sb("bq8", [P, NPAIR])
        bk = sb("bk", [P, NPAIR])
        gw8 = sb("gw8", [P, E])
        bo_col = sb("bo_col", [P, 1])
        gains = sb("gains", [P, 2])
        tg = sb("tg", [P, 2])
        stat = sb("stat", [P, NT, 6])
        mv_all = sb("mv_all", [P, NT, 2])
        var_eps = sb("var_eps", [P, NT])
        rstd = sb("rstd", [P, NT])
        nmax = sb("nmax", [P, PSLOT])
        psums = sb("psums", [P, PSLOT])
        rsum = sb("rsum", [P, PSLOT])
        ln_stat = sb("ln_stat", [P, CH, 6])
        ln_mv = sb("ln_mv", [P, CH, 2])
        ln_var = sb("ln_var", [P, CH])
        ln_rstd = sb("ln_rstd", [P, CH])
        minus_half = sb("minus_half", [P, NT])

        gu_w = [v.rearrange("p (s f) -> p s f", s=2) for v in (cT[:, :, :].rearrange("p s t -> p (s t)")[:, 0:2 * FPAD],
                wqk[:, :, :, :].rearrange("p w s n -> p (w s n)")[:, 0:2 * FPAD])]
        stage = pT[:, :, :, :, :].rearrange("p a b c s -> p (a b c s)")
        raw_w = stage[:, 0:3 * HD].rearrange("p (w n) -> p w n", w=3)
        raw_mk = stage[:, 3 * HD:4 * HD]
        raw_wo = stage[:, 4 * HD:5 * HD].rearrange("p (j d) -> p j d", j=NPAIR)
        gw_row = stage[0:E, 5 * HD:5 * HD + D]
        brows = stage[0:NPAIR, 5 * HD + D:5 * HD + D + 2 * P].rearrange("j (n p) -> j n p", n=2)
        ctx_tok = ffn_work[:, 0:TOK]
        raw_gu = ffn_work[:, :].rearrange("p (w f) -> p w f", w=2)
        flat_probs = probs[:, :, :].rearrange("p a b -> p (a b)")
        cT_route = flat_probs[:, TOK // 2:TOK // 2 + BLK // 2].bitcast(BF16)
        parts_blk = flat_probs[:, TOK // 2 + BLK // 2:TOK].bitcast(BF16)[:, 0:BLK]
        sel_sb = flat_probs[:, TOK:TOK + FEX // 2].bitcast(BF16).rearrange("p (j f) -> p j f", j=NJE)
        raw_sel = (qk_pair[:, :, :, :].rearrange("p a b c -> p (a b c)").bitcast(F32)[:, 0:FEX]
                   .rearrange("p (j f) -> p j f", j=NJE))
        wd_raw = stage[:, TOK + FEX:TOK + FEX + NJ * D].rearrange("p (j d) -> p j d", j=NJ)
        wd_parts = [v[:, at:at + NJ * D].rearrange("p (j d) -> p j d", j=NJ) for v, at in (
            (mem_k[:, :, :, :].rearrange("p a b c -> p (a b c)"), 0), (k_st[:, :, :].rearrange("p a b -> p (a b)"), 6 * BLK))]
        xln = v_sb[:, :, :, :].rearrange("p a b c -> p (a b c)")

        banks = [es.enter_context(nc.psum_tensor(f"bank{i}", [P, 512], F32)) for i in range(8)]

        loads = sems("cleared x_in ctx_in wq_in wk_in wv_in mk_in mv_in bias_in gate_in gain_in ident_in bv_in wo_in bo_in "
                 "misc_in gu_in pad_done var_ready rstd_ready ln_ready ln_link tr_done hi_done lo_done "
                 "small_done small_copied wq_hi wk_hi wv_hi wo_hi w_lo tanh_done identb_done")
        NMK = NPAIR // 4
        NJOB = 2 * NBLK + NMK
        job_dst = ([cT[:, :, j * BLK:(j + 1) * BLK] for j in range(NBLK)]
                   + [mem_k[:, 4 * j:4 * j + 4, :, :].rearrange("p h s m -> p s h m") for j in range(NMK)]
                   + [xT[:, :, j * BLK:(j + 1) * BLK] for j in range(NBLK)])

        def job_ap(j, part):
            d = job_dst[j][:, part]
            bank = banks[j % 7][:, :]
            return d, bank.rearrange("p (h m) -> p h m", h=4) if NBLK <= j < NBLK + NMK else bank

        def prologue_sp(sp):
            sp.dma_start(x_tok[:, :].rearrange("p (i d) -> p i d", i=NT),
                         x.rearrange("b (i p) d -> p (b i) d", p=P)).then_inc(loads["x_in"], 16)
            sp.dma_start(ident[:, :], identity).then_inc(loads["ident_in"], 16)
            sp.dma_start(ctx_tok.rearrange("p (i d) -> p i d", i=NT),
                         ctx.rearrange("b (i p) d -> p (b i) d", p=P)).then_inc(loads["ctx_in"], 16)
            sp.dma_start(raw_mk, mk[0]).then_inc(loads["mk_in"], 16)
            sp.dma_start(mem_v[:, :], mv[0]).then_inc(loads["mv_in"], 16)
            sp.dma_start(raw_wo, wo.rearrange("(j p) n -> p j n", p=P)).then_inc(loads["wo_in"], 16)
            sp.wait_ge(loads["tr_done"], NBLK)
            sp.wait_ge(loads["pad_done"], 1)
            for w, (we, ws) in enumerate(((w_gate, sw_gate), (w_up, sw_up))):
                sp.dma_start(raw_gu[:, w, 0:FEX].rearrange("p (e f) -> p e f", e=E),
                             we.rearrange("e d f -> d e f")).then_inc(loads["gu_in"], 16)
                sp.dma_start(raw_gu[:, w, FEX:FALL], ws).then_inc(loads["gu_in"], 16)
            for s, n in (("mv_in", 1), ("wo_in", 1)):
                sp.wait_ge(loads[s], 16 * n)

        def prologue_act(act):
            for n, g in enumerate((g_xattn, g_ffn)):
                act.dma_start(gains[:, n:n + 1], g.partition_broadcast(P)).then_inc(loads["gain_in"], 16)
            act.dma_start(raw_w[:, 0, :], wq).then_inc(loads["wq_in"], 16)
            act.dma_start(raw_w[:, 1, :], wk).then_inc(loads["wk_in"], 16)
            act.dma_start(raw_w[:, 2, :], wv).then_inc(loads["wv_in"], 16)
            for n, b in enumerate((wq_b, wk_b)):
                act.dma_start(brows[:, n, :], b.rearrange("(j p) -> j p", p=P)).then_inc(loads["bias_in"], 16)
            act.dma_start(gw_row[:, :], gate_w).then_inc(loads["gate_in"], 16)
            act.dma_start(bv_bc[:, :], wv_b.partition_broadcast(P)).then_inc(loads["bv_in"], 16)
            act.dma_start(bo_col[:, :], wo_b.rearrange("(p a) -> p a", a=1)).then_inc(loads["bo_in"], 16)
            act.dma_start(iota_sb[:, :], iota).then_inc(loads["misc_in"], 16)

            def high(j):
                act.wait_ge(loads["tr_done"], j + 1)
                dst, src = job_ap(j, 0)
                nc.scalar.activation(dst, src, ACT.Copy).then_inc(loads["hi_done"], 1)

            def weight_high(w, sem):
                act.wait_ge(loads[("wq_in", "wk_in")[w]], 16)
                nc.scalar.activation(wqk[:, w, 0, :], raw_w[:, w, :], ACT.Copy,
                                     scale=QSCALE if w == 0 else 1.0).then_inc(loads[sem], 1)

            act.wait_ge(loads["gain_in"], 32)
            nc.scalar.activation(tg[:, :], gains[:, :], ACT.Tanh).then_inc(loads["tanh_done"], 1)
            for j in range(NBLK):
                high(j)
            weight_high(0, "wq_hi")
            weight_high(1, "wk_hi")
            act.wait_ge(loads["wv_in"], 16)
            nc.scalar.activation(wvs[:, 0, :], raw_w[:, 2, :], ACT.Copy).then_inc(loads["wv_hi"], 1)
            act.wait_ge(loads["wo_in"], 16)
            nc.scalar.activation(wo_sb[:, 0, :, :], raw_wo, ACT.Copy).then_inc(loads["wo_hi"], 1)
            for j in range(NBLK, NJOB):
                high(j)
            act.wait_ge(loads["small_done"], 1)
            nc.scalar.activation(bq8[:, :], banks[7][:, 0:NPAIR], ACT.Copy, scale=QSCALE).then_inc(loads["small_copied"], 1)
            nc.scalar.activation(bk[:, :], banks[7][:, NPAIR:2 * NPAIR], ACT.Copy).then_inc(loads["small_copied"], 1)
            nc.scalar.activation(gw8[:, :], banks[7][:, H:H + E], ACT.Copy).then_inc(loads["small_copied"], 1)
            for s, n in (("bv_in", 16), ("bo_in", 16), ("misc_in", 16), ("tanh_done", 1), ("small_copied", 3)):
                act.wait_ge(loads[s], n)

        def prologue_pool(pool):
            for t in (k_st[:, 0:2, KW:KPART].bitcast(F32), x_pad[:, 0:BLK], oT[:, :, :, :].bitcast(F32), nmax[:, :],
                      q_st[:, 2:SLOTS, :].bitcast(F32), k_st[:, 2:SLOTS, :].bitcast(F32),
                      stage[:, 5 * HD + D + 2 * P:4 * BB * TC * S]):
                nc.gpsimd.memset(t, 0.0).then_inc(loads["cleared"], 1)
            for t in (psums[:, :], rsum[:, :]):
                nc.gpsimd.memset(t, 1.0).then_inc(loads["cleared"], 1)
            nc.gpsimd.memset(minus_half[:, :], -0.5).then_inc(loads["cleared"], 1)
            nc.gpsimd.memset(probs[:, :, :], 0.0).then_inc(loads["cleared"], 1)
            pool.wait_ge(loads["cleared"], 11)
            pool.wait_ge(loads["var_ready"], 1)
            for j in range(NBLK):
                part = slice(j * CH, (j + 1) * CH)
                nc.gpsimd.tensor_tensor(rstd[:, part], var_eps[:, part], minus_half[:, part], ALU.pow).then_inc(loads["rstd_ready"], 1)
            pool.wait_ge(loads["tr_done"], NBLK)
            nc.gpsimd.memset(raw_gu[:, :, FALL:FPAD], 0.0).then_inc(loads["pad_done"], 1)
            pool.wait_ge(loads["ident_in"], 16)
            nc.gpsimd.tensor_copy(ident_b[:, :], ident[:, :]).then_inc(loads["identb_done"], 1)
            pool.wait_ge(loads["identb_done"], 1)
            pool.wait_ge(loads["pad_done"], 1)
            pool.wait_ge(loads["wk_hi"], 1)
            nc.gpsimd.tensor_tensor(wqk[:, 1, 1, :], raw_w[:, 1, :], wqk[:, 1, 0, :].bitcast(F32),
                                    ALU.subtract).then_inc(loads["w_lo"], 1)
            pool.wait_ge(loads["wv_hi"], 1)
            nc.gpsimd.tensor_tensor(wvs[:, 1, :], raw_w[:, 2, :], wvs[:, 0, :].bitcast(F32),
                                    ALU.subtract).then_inc(loads["w_lo"], 1)
            pool.wait_ge(loads["wo_hi"], 1)
            nc.gpsimd.tensor_tensor(wo_sb[:, 1, :, :], raw_wo, wo_sb[:, 0, :, :].bitcast(F32),
                                    ALU.subtract).then_inc(loads["w_lo"], 1)
            pool.wait_ge(loads["w_lo"], 4)

        def prologue_dve(dve):
            def low(j):
                dve.wait_ge(loads["hi_done"], j + 1)
                hi, src = job_ap(j, 0)
                lo, _ = job_ap(j, 1)
                nc.vector.tensor_tensor(lo, src, hi.bitcast(F32), ALU.subtract).then_inc(loads["lo_done"], 1)

            dve.wait_ge(loads["x_in"], 16)
            for i in range(NT):
                nc.vector.bn_stats(stat[:, i, :], x_tok[:, i * P:(i + 1) * P]).then_inc(loads["ln_link"], 1)
            for i in range(NT):
                dve.wait_ge(loads["ln_link"], i + 1)
                nc.vector.bn_aggr(mv_all[:, i, :], stat[:, i, :]).then_inc(loads["ln_link"], 1)
            dve.wait_ge(loads["ln_link"], 2 * NT)
            nc.vector.tensor_scalar(var_eps[:, :], mv_all[:, :, 1], EPS, None, ALU.add).then_inc(loads["var_ready"], 1)
            for i in range(NT):
                dve.wait_ge(loads["rstd_ready"], i // CH + 1)
                nc.vector.tensor_scalar(xln[:, i * P:(i + 1) * P], x_tok[:, i * P:(i + 1) * P], mv_all[:, i, 0:1],
                                        rstd[:, i:i + 1], ALU.subtract, ALU.mult).then_inc(loads["ln_ready"], 1)
            for j in range(NBLK):
                low(j)
            dve.wait_ge(loads["wq_hi"], 1)
            nc.vector.scalar_tensor_tensor(wqk[:, 0, 1, :], raw_w[:, 0, :], QSCALE, wqk[:, 0, 0, :].bitcast(F32),
                                           ALU.mult, ALU.subtract).then_inc(loads["w_lo"], 1)
            for j in range(NBLK, NJOB):
                low(j)
            dve.wait_ge(loads["lo_done"], NJOB)

        def prologue_pe(pe):
            pe.wait_ge(loads["ident_in"], 16)

            def transpose4(j, src, ready=None):
                if j >= 7:
                    pe.wait_ge(loads["lo_done"], j - 6)
                for i in range(4):
                    if ready is not None:
                        pe.wait_ge(loads[ready], 4 * (j - NBLK - NMK) + i + 1)
                    ins = nc.tensor.transpose(banks[j % 7][:, i * P:(i + 1) * P], src(i), ident[:, :])
                ins.then_inc(loads["tr_done"], 1)

            pe.wait_ge(loads["ctx_in"], 16)
            for j in range(NBLK):
                transpose4(j, lambda i: ctx_tok[:, (4 * j + i) * P:(4 * j + i + 1) * P])
            pe.wait_ge(loads["mk_in"], 16)
            for j in range(NMK):
                transpose4(NBLK + j, lambda i: raw_mk[:, (4 * j + i) * P:(4 * j + i + 1) * P])
            pe.wait_ge(loads["bias_in"], 32)
            pe.wait_ge(loads["gate_in"], 16)
            for n in range(2):
                nc.tensor.transpose(banks[7][:, n * NPAIR:(n + 1) * NPAIR], brows[:, n, :], ident[0:NPAIR, 0:NPAIR])
            nc.tensor.transpose(banks[7][:, H:H + E], gw_row[:, :], ident[0:E, 0:E]).then_inc(loads["small_done"], 1)
            for j in range(NBLK):
                transpose4(NBLK + NMK + j, lambda i: xln[:, (4 * j + i) * P:(4 * j + i + 1) * P], ready="ln_ready")

        att = sems("ctx_blk q_proj k_proj q_hi q_lo k_hi k_lo slot0 slot1 slot2 slot3 v_proj v_ready scored maxed exped "
                 "rsum_ready normed transposed pT_act pT_dve weighed o_hi o_ready projected attn_sb attn_tr x1_done "
                 "x2_copied stat_done aggr_done var_done rstd_done ln2_done ln2_tr ln2_hi ln2_lo logit route route_exp "
                 "combined dve_passed")
        mid = sems("gu_hi gu_lo wd_in wd_pad wd_hi wd_lo sel_in sel_done r_zero")
        slot_in = [f"slot{i}" for i in range(SLOTS)]
        ROUTE_OPS = 15
        SLOT_DMAS = 6
        LEAD = 2
        TURN = dict(ctx_blk=1, q_proj=NPAIR, k_proj=NPAIR, q_hi=NPAIR, q_lo=NPAIR, k_hi=NPAIR, k_lo=NPAIR,
                    v_proj=2 * NG, v_ready=2 * NG, scored=CH * H, maxed=CH * H, exped=CH * H, rsum_ready=CH * H,
                    normed=CH * H, transposed=CH * H, pT_act=(CH - 1) * H, pT_dve=H, weighed=2 * NPAIR,
                    o_hi=NPAIR, o_ready=NPAIR, projected=NPAIR, attn_sb=1, attn_tr=1, x1_done=1, x2_copied=1, stat_done=1,
                    aggr_done=1, var_done=1, rstd_done=1, ln2_done=1, ln2_tr=2, ln2_hi=2, ln2_lo=2, logit=1,
                    route=ROUTE_OPS, route_exp=1, combined=1, dve_passed=0,
                    **{s: SLOT_DMAS * 16 * H // SLOTS for s in slot_in})
        ready = es.enter_context(nc.semaphore("ready"))
        ring, bank_t = banks[0:RING], banks[RING:RING + NTB]
        bank_o, bank_y = banks[6], banks[7]
        key_chunk = [[(0, 0), (0, 1), None], [None, (1, 0), (1, 1)]]
        FREED = {"Q": "q_lo", "K": "k_lo", "V": "v_ready", "S": "exped", "Z": "x1_done", "L": "ln2_lo",
                 "G": "route"}
        PER = {"Q": NPAIR, "K": NPAIR, "V": 2 * NG, "S": CH * H, "Z": 1, "L": 2, "G": 1}
        pe_turn, act_turn, dve_turn, pool_turn = (turn(SCHED[e]) for e in ("pe", "act", "dve", "pool"))
        jobs = [(t, i) for t, i in pe_turn if t in PER]
        place = {(t, i % PER[t]): at % RING for at, (t, i) in enumerate(jobs)}
        assert len(jobs) % RING == 0 and len(jobs) == sum(PER.values())

        def bank_of(kind, i):
            return ring[place[kind, i % PER[kind]]]

        def late(tasks, kinds):
            return sum(t in kinds and i < 0 for t, i in tasks)

        MADE = dict(scored=(pe_turn, "S"), transposed=(pe_turn, "T"), weighed=(pe_turn, "W"), projected=(pe_turn, "O"),
                    attn_tr=(pe_turn, "Z"), maxed=(dve_turn, "M"), rsum_ready=(dve_turn, "I"), pT_dve=(dve_turn, "D"),
                    x1_done=(dve_turn, "X"), exped=(act_turn, "E"), pT_act=(act_turn, "A"), o_hi=(act_turn, "P"),
                    o_ready=(dve_turn, "P"),
                    attn_sb=(act_turn, "Y"), stat_done=(dve_turn, "N"), aggr_done=(dve_turn, "G"),
                    var_done=(dve_turn, "F"), rstd_done=(pool_turn, "R"), ln2_done=(dve_turn, "U"), ln2_tr=(pe_turn, "L"),
                    ln2_hi=(act_turn, "L"), ln2_lo=(dve_turn, "L"), logit=(pe_turn, "G"),
                    x2_copied=(dve_turn, "R"), route_exp=(act_turn, "X"), normed=(pool_turn, "C"))
        def late_events(name):
            if name in ("route", "combined"):
                return TURN[name]
            return late(*MADE[name]) if name in MADE else 0

        assert late(dve_turn, "H") == 4 and late(act_turn, "X") == 1
        assert not any(late(t, "QKVB") for t in (pe_turn, act_turn, dve_turn))

        def waiter(eng, blk):
            def done(name, i, each=1):
                eng.wait_ge(att[name], (blk + LEAD) * TURN[name] + (i + 1) * each)
            return done

        def turns(eng, tasks, do, before={}):
            with eng.Fori(0, NBLK) as blk:
                for t, i in tasks:
                    do(blk, waiter(eng, blk), t, i)
            for t, i in tasks:
                if i < 0:
                    if (t, i) in before:
                        before[t, i]()
                    do(NBLK, waiter(eng, NBLK), t, i)

        def over(eng, name):
            eng.wait_ge(att[name], (NBLK + LEAD) * TURN[name])

        lg, pr, i8, hit1 = (route_work[:, k * CH * E:(k + 1) * CH * E].rearrange("p (i e) -> p i e", i=CH) for k in range(4))
        m8, hit0 = lg, i8
        i8 = i8.bitcast(U32)
        idf = route_work[:, 4 * CH * E:4 * CH * E + CH * TOPK].rearrange("p (i k) -> p i k", i=CH)
        red = route_work[:, 4 * CH * E + CH * TOPK:].rearrange("p (k i) -> p k i", k=4)

        def part_ap(i):
            return parts_blk.rearrange("p (i k) -> p i k", i=CH)[:, :, i * PART:i * PART + E]

        SPLIT_OPS = 4
        ffn = sems("gated upped routed silued hid_up hid_all hid_hi hid_lo down y_sb y_tr y_out stored "
                   "split fetched parts_tr cT_ready")
        FTURN = dict(gated=NJ, upped=NJ, routed=NJE, silued=NJ, hid_up=NJ, hid_all=NJE, hid_hi=NJ, hid_lo=NJ, down=NJ,
                     y_sb=1, y_tr=1, y_out=1, stored=16, split=SPLIT_OPS, fetched=1, parts_tr=1, cT_ready=1)
        bank_g, bank_u, bank_c = banks[4:6], banks[6:8], banks[0:2]
        bank_d, bank_z = banks[2], banks[3]
        sil = ffn_work[:, 0:2 * BLK].rearrange("p (s t) -> p s t", s=2)
        hid = ffn_work[:, 2 * BLK:5 * BLK].rearrange("p (s t) -> p s t", s=3)
        yT = ffn_work[:, 5 * BLK:6 * BLK]
        res = ffn_work[:, 6 * BLK:7 * BLK]
        hid_parts = (k_st[:, :, :].rearrange("p a b -> p (a b)")[:, 0:6 * BLK]
                     .rearrange("p (s r t) -> p s r t", s=3, r=2))
        out_blk = out.rearrange("b s d -> (b s) d").rearrange("(n i p) d -> n p i d", n=NBLK, p=P)
        tasks = {e: fturn(FSCHED[e]) for e in FSCHED}
        FMADE = dict(down=("pe", "D"), y_tr=("pe", "Z"), silued=("act", "L"), hid_hi=("act", "A"), y_sb=("act", "Y"),
                     hid_up=("dve", "H"), hid_all=("dve", "N"), y_out=("dve", "X"), hid_lo=("pool", "B"),
                     gated=("pe", "G"), upped=("pe", "U"), routed=("pe", "R"),
                     fetched=("dve", "F"), parts_tr=("pe", "P"), cT_ready=("dve", "C"))

        def in_order(lates):
            return all(m <= n for m, n in zip(lates, lates[1:]))

        assert in_order([late(dve_turn, "M"), late(act_turn, "E")])
        assert in_order([late(act_turn, "P"), late(dve_turn, "P")])
        assert in_order([late(tasks[e], k) for e, k in (("pe", "U"), ("dve", "H"), ("act", "A"), ("pool", "B"), ("pe", "D"))])

        def fturn_waiter(eng, blk):
            def done(sem, i, each=1):
                eng.wait_ge(ffn[sem], (blk + LEAD) * FTURN[sem] + (i + 1) * each)
            return done

        def fturns(eng, name, do, begun=()):
            apart = 1 if begun else 0
            for t, i in tasks[name] * apart:
                if (t, i) not in begun:
                    do(0, fturn_waiter(eng, 0), t, i)
            with eng.Fori(apart, NBLK) as blk:
                for t, i in tasks[name]:
                    do(blk, fturn_waiter(eng, blk), t, i)
            for t, i in tasks[name]:
                if i < 0:
                    do(NBLK, fturn_waiter(eng, NBLK), t, i)

        def chunk(j):
            return (j % NJ + NJE) % NJ

        def of_routed(r):
            return r + NSH if r >= 0 else r

        def whole(done, j):
            k = j % NJ - NSH
            if k >= 0:
                done("hid_all", k - (0 if j >= 0 else NJE))
            else:
                done("hid_up", j)

        def slot(j):
            return j % NJ % 3

        def freed(done, sem, j):
            k = j % NJ
            done(sem, j - 3 if k >= 3 else j - k - NJ + max(m for m in range(NJ) if m % 3 == k))

        with nc.Block() as block:
            @block.sync
            def _(sp):
                prologue_sp(sp)
                for name in att:
                    if TURN[name]:
                        sp.sem_inc(att[name], LEAD * TURN[name] - late_events(name))
                for name in ffn:
                    made = FMADE.get(name)
                    sp.sem_inc(ffn[name], LEAD * FTURN[name] - (late(tasks[made[0]], made[1]) if made else 0))
                sp.sem_inc(ready, 1)
                sp.wait_ge(ready, 5)
                with sp.Fori(0, NBLK) as blk:
                    done = waiter(sp, blk)
                    for h in range(H):
                        p, hh = h // 2, h % 2
                        rows = slice(hh * DK, (hh + 1) * DK)
                        sem = att[slot_in[h % SLOTS]]
                        done("scored", CH * (h - SLOTS) + CH - 1)
                        for r in range(2):
                            k = k_st[r * DK:(r + 1) * DK, h % SLOTS, S:S + MEM]
                            dst = bass.AP(k.tensor, k.offset, [list(k.ap[0]), [KPART, 2], [1, MEM]])
                            sp.dma_start(dst.bitcast(F32), mem_k[rows, p, :, :].bitcast(F32)).then_inc(sem, 16)
                        done("q_lo", p)
                        for part in range(2):
                            sp.dma_start(q_st[part * DK:(part + 1) * DK, h % SLOTS, :].bitcast(F32),
                                         qk_pair[rows, 0, part, :].bitcast(F32)).then_inc(sem, 16)
                        done("k_lo", p)
                        for r in range(2):
                            k = k_st[r * DK:(r + 1) * DK, h % SLOTS, :]
                            dst = bass.AP(k.tensor, k.offset, [list(k.ap[0]), [S + MEM, 2 * BB], [1, S]]).bitcast(F32)
                            src = qk_pair[rows, 1, :, :].bitcast(F32).rearrange("p s (b t) -> p (s b) t", b=BB)
                            sp.dma_start(dst, src).then_inc(sem, 16)
                for s in slot_in:
                    over(sp, s)
                sp.dma_start(raw_sel, selector).then_inc(mid["sel_in"], 16)
                over(sp, "weighed")
                sp.dma_start(wd_raw[:, 0:NJE, :], w_down.rearrange("e f d -> (e f) d")
                             .rearrange("(j p) d -> p j d", p=P)).then_inc(mid["wd_in"], 16)
                sp.dma_start(wd_raw[:, NJE:NJ - 1, :], sw_down[0:(NJ - 1 - NJE) * P, :]
                             .rearrange("(j p) d -> p j d", p=P)).then_inc(mid["wd_in"], 16)
                sp.wait_ge(mid["wd_pad"], 1)
                sp.dma_start(wd_raw[0:LAST, NJ - 1, :], sw_down[(NJ - 1 - NJE) * P:FS, :]).then_inc(mid["wd_in"], 16)
                with sp.Fori(0, NBLK) as blk:
                    fturn_waiter(sp, blk)("y_out", 0)
                    sp.dma_start(out_blk[blk], res.rearrange("p (i d) -> p i d", i=CH)).then_inc(ffn["stored"], 16)
                sp.wait_ge(ffn["stored"], (NBLK + LEAD) * FTURN["stored"])

            @block.tensor
            def _(pe):
                prologue_pe(pe)
                pe.sem_inc(ready, 1)
                pe.wait_ge(ready, 5)
                nc.tensor.matmul(bank_y[:, :], x_pad[:, 0:P], x_pad[:, 0:BLK], start=True, stop=False)

                def take(blk, done, kind, i):
                    at = jobs.index((kind, i)) - RING
                    while isinstance(blk, int) and at >= 0 and jobs[at][1] >= 0:
                        at -= RING
                    k, m = jobs[at]
                    m -= PER[k] if at < 0 else 0
                    done(FREED[k], ROUTE_OPS * m + 1 if k == "G" else m)
                    return bank_of(kind, i)

                def project(blk, done, which, p):
                    bank = take(blk, done, "QK"[which], p)
                    for n, (ws, xs) in enumerate(((0, 0), (0, 1), (1, 0))):
                        ins = nc.tensor.matmul(bank[:, :], wqk[:, which, ws, p * P:(p + 1) * P],
                                               (xT, cT)[which][:, xs, bass.ts(blk, BLK)], start=(n == 0), stop=(n == 2))
                    ins.then_inc(att[("q_proj", "k_proj")[which]], 1)

                def values(blk, done, i):
                    g, half = divmod(i, 2)
                    bank = take(blk, done, "V", i)
                    done("ctx_blk", 0)
                    for c2 in range(2):
                        c = 2 * half + c2
                        for n, (cs, ws) in enumerate(((0, 0), (0, 1), (1, 0))):
                            ins = nc.tensor.matmul(bank[:, c2 * GW:(c2 + 1) * GW], cT_blk[:, cs, c * P:(c + 1) * P],
                                                   wvs[:, ws, g * GW:(g + 1) * GW], start=(n == 0), stop=(n == 2))
                    ins.then_inc(att["v_proj"], 1)

                def scores(blk, done, n):
                    h, c = divmod(n, CH)
                    if c == 0:
                        done(slot_in[h % SLOTS], h // SLOTS, SLOT_DMAS * 16)
                    bank = take(blk, done, "S", n)
                    at = S * (c // 2)
                    for part in range(2):
                        ins = nc.tensor.matmul(bank[:, 0:T], q_st[:, h % SLOTS, c * P:(c + 1) * P],
                                               k_st[:, h % SLOTS, part * KPART + at:part * KPART + at + T],
                                               start=(part == 0), stop=(part == 1))
                    ins.then_inc(att["scored"], 1)

                def transpose(done, n):
                    done("normed", n)
                    h, c = divmod(n - NTB, CH)
                    if c < CH - 1:
                        done("pT_act", (CH - 1) * h + c)
                    else:
                        done("pT_dve", h)
                    for t in range(TC):
                        ins = nc.tensor.transpose(bank_t[n % NTB][:, t * P:(t + 1) * P],
                                                  probs[:, n % PSLOT, t * P:(t + 1) * P], ident[:, :])
                    ins.then_inc(att["transposed"], 1)

                def weigh(done, i):
                    p, bb = divmod(i, 2)
                    done("pT_act", (CH - 1) * (2 * p + 2) - 1)
                    done("pT_dve", 2 * p + 1)
                    if bb == 0:
                        done("o_ready", p - 1)
                    for t in range(TC):
                        for hh in range(2):
                            h = (2 * p + hh) % H
                            where = key_chunk[bb][t]
                            if where is None:
                                vals = mem_v[:, h * DK:(h + 1) * DK]
                            else:
                                vals = v_sb[:, (h // GH) % 2, 2 * where[0] + where[1], (h % GH) * DK:(h % GH + 1) * DK]
                            ins = nc.tensor.matmul(bank_o[hh * DK:(hh + 1) * DK, bb * S:(bb + 1) * S], vals,
                                                   pT[:, h % 4, bb, t, :], start=(t == 0), stop=(t == TC - 1))
                    ins.then_inc(att["weighed"], 1)

                def project_out(done, p):
                    done("o_ready", p)
                    if p % NPAIR == 0:
                        done("attn_sb", -1)
                    for n, (ws, os) in enumerate(((0, 0), (1, 0), (0, 1))):
                        ins = nc.tensor.matmul(bank_y[:, :], wo_sb[:, ws, p % NPAIR, :], oT[:, p % 2, os, :],
                                               start=(p % NPAIR == 0 and n == 0), stop=(p % NPAIR == NPAIR - 1 and n == 2))
                    ins.then_inc(att["projected"], 1)

                def turn_back(blk, done, i):
                    done("attn_sb", i)
                    bank = take(blk, done, "Z", i)
                    for c in range(CH):
                        ins = nc.tensor.transpose(bank[:, c * P:(c + 1) * P], x2ln[:, c * P:(c + 1) * P], ident[:, :])
                    ins.then_inc(att["attn_tr"], 1)

                def do(blk, done, t, i):
                    if t == "S": scores(blk, done, i)
                    if t == "T": transpose(done, i)
                    if t == "Q": project(blk, done, 0, i)
                    if t == "K": project(blk, done, 1, i)
                    if t == "V": values(blk, done, i)
                    if t == "W": weigh(done, i)
                    if t == "O": project_out(done, i)
                    if t == "Z": turn_back(blk, done, i)
                    if t == "L": ln2_back(blk, done, i)
                    if t == "G": logits(blk, done, i)

                def ln2_back(blk, done, i):
                    if i % 2 == 0:
                        done("ln2_done", -1)
                    bank = take(blk, done, "L", i)
                    for c in range(2):
                        at = (2 * (i % 2) + c) * P
                        ins = nc.tensor.transpose(bank[:, c * P:(c + 1) * P], x2ln[:, at:at + P], ident[:, :])
                    ins.then_inc(att["ln2_tr"], 1)

                def logits(blk, done, i):
                    done("ln2_hi", 2 * i + 1)
                    bank = take(blk, done, "G", i)
                    for c in range(CH):
                        ins = nc.tensor.matmul(bank[:, c * E:(c + 1) * E], x2ln[:, c * P:(c + 1) * P], gw8[:, :],
                                               start=True, stop=True)
                    ins.then_inc(att["logit"], 1)

                def up(blk, done, w, j):
                    done(("silued", "hid_up")[w], j - 2)
                    bank = (bank_g, bank_u)[w][j % 2]
                    for n, (ws, xs) in enumerate(((0, 0), (0, 1), (1, 0))):
                        ins = nc.tensor.matmul(bank[:, :], gu_w[w][:, ws, chunk(j) * P:(chunk(j) + 1) * P],
                                               xT[:, xs, bass.ts(blk, BLK)], start=(n == 0), stop=(n == 2))
                    ins.then_inc(ffn[("gated", "upped")[w]], 1)

                begun = ([("G", j) for j in range(2 - late(tasks["act"], "L"))]
                         + [("U", j) for j in range(2 - late(tasks["dve"], "H"))])

                def first_chunks():
                    for name in ("pT_act", "pT_dve", "o_ready", "attn_sb"):
                        over(pe, name)
                    pe.wait_ge(mid["gu_lo"], 2)
                    for t, j in begun:
                        up(0, fturn_waiter(pe, 0), "GU".index(t), j)

                turns(pe, pe_turn, do, before={("L", -2): first_chunks})
                for name in ("q_lo", "k_lo", "v_ready", "exped", "x1_done", "ln2_lo"):
                    over(pe, name)
                waiter(pe, NBLK)("route", 1 - ROUTE_OPS)
                nc.tensor.matmul(bank_d[:, :], x_pad[:, 0:P], x_pad[:, 0:BLK], start=True, stop=False)

                def route(blk, done, r):
                    done("cT_ready", 0)
                    done("hid_all", r - 2 if r >= 2 else -1)
                    nc.tensor.matmul(bank_c[r % 2][:, :], sel_sb[:, r, :], cT_route,
                                     start=True, stop=True).then_inc(ffn["routed"], 1)

                def down(done, j):
                    if j < 0:
                        pe.wait_ge(mid["wd_lo"], 1)
                    done("hid_lo", j)
                    if j % NJ == 0:
                        done("y_sb", -1)
                    for n, (ws, hs) in enumerate(((0, 0), (1, 0), (0, 1))):
                        ins = nc.tensor.matmul(bank_d[:, :], wd_parts[ws][:, chunk(j), :], hid_parts[:, slot(j), hs, :],
                                               start=(j % NJ == 0 and n == 0), stop=(j % NJ == NJ - 1 and n == 2))
                    ins.then_inc(ffn["down"], 1)

                def output_back(blk, done):
                    done("y_sb", -1)
                    done("cT_ready", 0 if z_behind_p and not (isinstance(blk, int) and blk == NBLK) else -1)
                    for c in range(CH):
                        ins = nc.tensor.transpose(bank_z[:, c * P:(c + 1) * P], yT[:, c * P:(c + 1) * P], ident[:, :])
                    ins.then_inc(ffn["y_tr"], 1)

                z_behind_p = tasks["pe"].index(("Z", -1)) > tasks["pe"].index(("P", 0))

                def weights_back(done, i):
                    done("fetched", i)
                    done("y_out", -2 if z_behind_p else -1)
                    for c in range(CH):
                        ins = nc.tensor.transpose(bank_z[:, 0:BLK // 2].bitcast(BF16)[:, c * P:(c + 1) * P],
                                                  parts_blk[:, c * P:(c + 1) * P], ident_b[:, :])
                    ins.then_inc(ffn["parts_tr"], 1)

                def ffn_do(blk, done, t, i):
                    if t == "G": up(blk, done, 0, i)
                    if t == "U": up(blk, done, 1, i)
                    if t == "R": route(blk, done, i)
                    if t == "D": down(done, i)
                    if t == "P": weights_back(done, i)
                    if t == "Z": output_back(blk, done)

                fturns(pe, "pe", ffn_do, begun)

            @block.scalar
            def _(act):
                prologue_act(act)
                act.sem_inc(ready, 1)
                act.wait_ge(ready, 5)

                def high(done, which, p):
                    done(("q_proj", "k_proj")[which], p)
                    for h in (2 * p - 2, 2 * p - 1):
                        done(slot_in[h % SLOTS], h // SLOTS, SLOT_DMAS * 16)
                    nc.scalar.activation(qk_pair[:, which, 0, :], bank_of("QK"[which], p)[:, :], ACT.Identity,
                                         bias=(bq8, bk)[which][:, p:p + 1]).then_inc(att[("q_hi", "k_hi")[which]], 1)

                def exps(done, n):
                    done("maxed", n)
                    done("transposed", n - PSLOT)
                    j = n % PSLOT
                    nc.scalar.activation(probs[:, j, :], bank_of("S", n)[:, 0:T], ACT.Exp, bias=nmax[:, j:j + 1],
                                         accum_out=psums[:, j:j + 1]).then_inc(att["exped"], 1)

                def copy_out(done, i):
                    h, c = divmod(i, CH - 1)
                    done("transposed", CH * h + c)
                    done("weighed", 2 * (h // 2 - 2) + 1)
                    nc.scalar.activation(pT[:, h % 4, c // 2, :, (c % 2) * P:(c % 2 + 1) * P],
                                         bank_t[c % NTB][:, 0:T].rearrange("p (t s) -> p t s", t=TC), ACT.Copy).then_inc(att["pT_act"], 1)

                def pair_out(done, p):
                    done("weighed", 2 * p + 1)
                    done("projected", p - 2)
                    nc.scalar.activation(oT[:, p % 2, 0, :], bank_o[:, :], ACT.Copy).then_inc(att["o_hi"], 1)

                def add_bias(done, i):
                    done("projected", (i + 1) * NPAIR - 1)
                    done("logit", i - 1)
                    nc.scalar.activation(x2ln[:, :], bank_y[:, :], ACT.Identity, bias=bo_col[:, 0:1]).then_inc(att["attn_sb"], 1)

                def do(blk, done, t, i):
                    if t == "E": exps(done, i)
                    if t == "A": copy_out(done, i)
                    if t == "Q": high(done, 0, i)
                    if t == "K": high(done, 1, i)
                    if t == "P": pair_out(done, i)
                    if t == "Y": add_bias(done, i)
                    if t == "L": ln2_high(blk, done, i)
                    if t == "X": route_exp(done, i)

                def ln2_high(blk, done, i):
                    done("ln2_tr", i)
                    half = bass.ds(blk * BLK + i % 2 * 2 * P, 2 * P)
                    nc.scalar.activation(x2ln[:, i % 2 * 2 * P:(i % 2 + 1) * 2 * P], bank_of("L", i)[:, 0:2 * P], ACT.Copy)
                    nc.scalar.activation(xT_pad[:, 0, half], bank_of("L", i)[:, 0:2 * P], ACT.Copy).then_inc(att["ln2_hi"], 1)

                def route_exp(done, i):
                    done("route", ROUTE_OPS * i + 1)
                    nc.scalar.activation(pr[:, :, :], lg[:, :, :], ACT.Exp).then_inc(att["route_exp"], 1)

                def gate_up_high():
                    act.wait_ge(loads["gu_in"], 64)
                    over(act, "ctx_blk")
                    over(act, "q_proj")
                    over(act, "k_proj")
                    for w in range(2):
                        nc.scalar.activation(gu_w[w][:, 0, :], raw_gu[:, w, :], ACT.Copy).then_inc(mid["gu_hi"], 1)

                def down_high():
                    act.wait_ge(mid["sel_in"], 16)
                    nc.scalar.activation(sel_sb, raw_sel, ACT.Copy).then_inc(mid["sel_done"], 1)
                    act.wait_ge(mid["wd_in"], 48)
                    for s in slot_in:
                        over(act, s)
                    nc.scalar.activation(wd_parts[0], wd_raw, ACT.Copy).then_inc(mid["wd_hi"], 1)

                turns(act, act_turn, do, before={("P", -1): gate_up_high, ("L", -2): down_high})
                act.wait_ge(mid["gu_lo"], 2)

                def ffn_do(blk, done, t, i):
                    if t == "L":
                        done("gated", i)
                        done("hid_up", i - 2)
                        nc.scalar.activation(sil[:, i % 2, :], bank_g[i % 2][:, :], ACT.Silu).then_inc(ffn["silued"], 1)
                    if t == "A":
                        whole(done, i)
                        freed(done, "down", i)
                        nc.scalar.activation(hid_parts[:, slot(i), 0, :], hid[:, slot(i), :], ACT.Copy).then_inc(ffn["hid_hi"], 1)
                    if t == "Y":
                        done("down", -1)
                        done("y_tr", -2)
                        nc.scalar.activation(yT, bank_d[:, :], ACT.Copy).then_inc(ffn["y_sb"], 1)

                fturns(act, "act", ffn_do)

            @block.vector
            def _(dve):
                prologue_dve(dve)
                dve.sem_inc(ready, 1)
                dve.wait_ge(ready, 5)

                def low(done, which, p):
                    done(("q_hi", "k_hi")[which], p)
                    nc.vector.scalar_tensor_tensor(qk_pair[:, which, 1, :], bank_of("QK"[which], p)[:, :],
                                                   (bq8, bk)[which][:, p:p + 1], qk_pair[:, which, 0, :].bitcast(F32),
                                                   ALU.add, ALU.subtract).then_inc(att[("q_lo", "k_lo")[which]], 1)

                def maximum(done, n):
                    done("scored", n)
                    j = n % PSLOT
                    nc.vector.tensor_reduce(nmax[:, j:j + 1], bank_of("S", n)[:, 0:T], axis=AX.X, op=ALU.max,
                                            negate=True).then_inc(att["maxed"], 1)

                def inverse(done, n):
                    done("exped", n)
                    j = n % PSLOT
                    nc.vector.reciprocal(rsum[:, j:j + 1], psums[:, j:j + 1]).then_inc(att["rsum_ready"], 1)

                def copy_out(done, h):
                    c = CH - 1
                    done("transposed", CH * h + c)
                    done("weighed", 2 * (h // 2 - 2) + 1)
                    nc.vector.tensor_copy(pT[:, h % 4, c // 2, :, (c % 2) * P:(c % 2 + 1) * P],
                                          bank_t[c % NTB][:, 0:T].rearrange("p (t s) -> p t s", t=TC)).then_inc(att["pT_dve"], 1)

                def pair_low(done, p):
                    done("o_hi", p)
                    nc.vector.tensor_tensor(oT[:, p % 2, 1, :], bank_o[:, :], oT[:, p % 2, 0, :].bitcast(F32),
                                            ALU.subtract).then_inc(att["o_ready"], 1)

                def values_out(done, i):
                    g, half = divmod(i, 2)
                    done("v_proj", i)
                    done("weighed", 2 * (g - 1) * (GH // 2) - 1)
                    bias = bv_bc[:, g * GW:(g + 1) * GW].unsqueeze(1).broadcast_to([P, 2, GW])
                    nc.vector.tensor_tensor(v_sb[:, g % 2, 2 * half:2 * half + 2, :],
                                            bank_of("V", i)[:, :].rearrange("p (c n) -> p c n", c=2),
                                            bias, ALU.add).then_inc(att["v_ready"], 1)

                def fetch_ctx(blk, done, i):
                    done("v_proj", 2 * NG * i - 1)
                    nc.vector.tensor_copy(cT_blk[:, :, :], cT[:, :, bass.ts(blk, BLK)].bitcast(F32)).then_inc(att["ctx_blk"], 1)

                def ln2_fetch(blk, done, i):
                    done("logit", i - 1)
                    done("x1_done", i)
                    passing()
                    nc.vector.tensor_copy(x2ln[:, :], x_pad[:, bass.ts(blk, BLK)]).then_inc(att["x2_copied"], 1)

                def passing():
                    nc.vector.sem_inc(att["dve_passed"], 1)

                def ln2_stats(done, i):
                    done("x2_copied", i)
                    passing()
                    for c in range(CH):
                        ins = nc.vector.bn_stats(ln_stat[:, c, :], x2ln[:, c * P:(c + 1) * P])
                    ins.then_inc(att["stat_done"], 1)

                def ln2_aggregate(done, i):
                    done("stat_done", i)
                    passing()
                    for c in range(CH):
                        ins = nc.vector.bn_aggr(ln_mv[:, c, :], ln_stat[:, c, :])
                    ins.then_inc(att["aggr_done"], 1)

                def ln2_variance(done, i):
                    done("aggr_done", i)
                    done("rstd_done", i - 1)
                    nc.vector.tensor_scalar(ln_var[:, :], ln_mv[:, :, 1], EPS, None, ALU.add).then_inc(att["var_done"], 1)

                def ln2_apply(done, i):
                    done("rstd_done", i)
                    for c in range(CH):
                        xs = x2ln[:, c * P:(c + 1) * P]
                        ins = nc.vector.tensor_scalar(xs, xs, ln_mv[:, c, 0:1], ln_rstd[:, c:c + 1], ALU.subtract, ALU.mult)
                    ins.then_inc(att["ln2_done"], 1)

                def ln2_low(blk, done, i):
                    done("ln2_hi", i)
                    half = bass.ds(blk * BLK + i % 2 * 2 * P, 2 * P)
                    nc.vector.tensor_tensor(xT_pad[:, 1, half], bank_of("L", i)[:, 0:2 * P],
                                            xT_pad[:, 0, half].bitcast(F32), ALU.subtract).then_inc(att["ln2_lo"], 1)

                def route(blk, done, i):
                    at = ROUTE_OPS * (i // 4)

                    def behind(k):
                        done("route", at + k - 1)

                    def link(ins):
                        ins.then_inc(att["route"], 1)

                    def over_e(v):
                        return v.unsqueeze(2).broadcast_to([P, CH, E])

                    if i % 4 == 0:
                        done("logit", i // 4)
                        logits = bank_of("G", i // 4)[:, 0:CH * E].rearrange("p (i e) -> p i e", i=CH)
                        link(nc.vector.tensor_reduce(red[:, 0, :], logits, axis=AX.X, op=ALU.max))
                        behind(1)
                        link(nc.vector.tensor_tensor(lg, logits, over_e(red[:, 0, :]), ALU.subtract))
                    if i % 4 == 1:
                        done("route_exp", i // 4)
                        link(nc.vector.tensor_reduce(red[:, 1, :], pr, axis=AX.X, op=ALU.add))
                        behind(3)
                        link(nc.vector.reciprocal(red[:, 2, :], red[:, 1, :]))
                        behind(4)
                        link(nc.vector.tensor_tensor(pr, pr, over_e(red[:, 2, :]), ALU.mult))
                    if i % 4 == 2:
                        behind(5)
                        passing()
                        for c in range(CH):
                            ins = nc.vector.max(m8[:, c, :], pr[:, c, :])
                        link(ins)
                        behind(6)
                        passing()
                        for c in range(CH):
                            ins = nc.vector.max_index(i8[:, c, :], m8[:, c, :], pr[:, c, :])
                        link(ins)
                        behind(7)
                        passing()
                        link(nc.vector.tensor_copy(idf, i8[:, :, 0:TOPK]))
                        link(nc.vector.tensor_tensor(red[:, 3, :], m8[:, :, 0], m8[:, :, 1], ALU.add))
                    if i % 4 == 3:
                        behind(9)
                        link(nc.vector.tensor_scalar(red[:, 3, :], red[:, 3, :], 1e-20, None, ALU.add))
                        behind(10)
                        link(nc.vector.reciprocal(red[:, 0, :], red[:, 3, :]))
                        for k, hit in enumerate((hit0, hit1)):
                            link(nc.vector.tensor_tensor(hit, iota_sb[:, :].unsqueeze(1).broadcast_to([P, CH, E]),
                                                         over_e(idf[:, :, k]), ALU.is_equal))
                        behind(13)
                        link(nc.vector.tensor_tensor(hit0, hit0, hit1, ALU.add))
                        link(nc.vector.tensor_tensor(pr, pr, over_e(red[:, 0, :]), ALU.mult))
                        behind(15)
                        nc.vector.scalar_tensor_tensor(
                            comb_pad[:, bass.ts(blk, CH * E)].rearrange("p (i e) -> p i e", i=CH), pr, ROUTE_SCALE, hit0,
                            ALU.mult, ALU.mult).then_inc(att["combined"], 1)

                def gate_low():
                    dve.wait_ge(mid["gu_hi"], 1)
                    nc.vector.tensor_tensor(gu_w[0][:, 1, :], raw_gu[:, 0, :], gu_w[0][:, 0, :].bitcast(F32),
                                            ALU.subtract).then_inc(mid["gu_lo"], 1)

                def residual(blk, done, i):
                    done("attn_tr", i)
                    xs = x_pad[:, bass.ts(blk, BLK)]
                    nc.vector.scalar_tensor_tensor(xs, bank_of("Z", i)[:, :], tg[:, 0:1], xs, ALU.mult, ALU.add).then_inc(att["x1_done"], 1)

                def do(blk, done, t, i):
                    if t == "M": maximum(done, i)
                    if t == "I": inverse(done, i)
                    if t == "D": copy_out(done, i)
                    if t == "Q": low(done, 0, i)
                    if t == "K": low(done, 1, i)
                    if t == "V": values_out(done, i)
                    if t == "B": fetch_ctx(blk, done, i)
                    if t == "X": residual(blk, done, i)
                    if t == "P": pair_low(done, i)
                    if t == "R": ln2_fetch(blk, done, i)
                    if t == "N": ln2_stats(done, i)
                    if t == "G": ln2_aggregate(done, i)
                    if t == "F": ln2_variance(done, i)
                    if t == "U": ln2_apply(done, i)
                    if t == "L": ln2_low(blk, done, i)
                    if t == "H": route(blk, done, i)

                turns(dve, dve_turn, do, before={("X", -1): gate_low})
                over(dve, "combined")
                dve.wait_ge(mid["r_zero"], 1)
                dve.wait_ge(mid["gu_lo"], 2)

                def ffn_do(blk, done, t, i):
                    if t == "H":
                        done("silued", i)
                        done("upped", i)
                        freed(done, "hid_lo", i)
                        nc.vector.tensor_tensor(hid[:, slot(i), :], bank_u[i % 2][:, :], sil[:, i % 2, :],
                                                ALU.mult).then_inc(ffn["hid_up"], 1)
                    if t == "N":
                        done("routed", i)
                        done("hid_up", of_routed(i))
                        h = hid[:, slot(of_routed(i)), :]
                        nc.vector.tensor_tensor(h, bank_c[i % NJE % 2][:, :], h, ALU.mult).then_inc(ffn["hid_all"], 1)
                    if t == "F":
                        done("parts_tr", i - 1)
                        comb = comb_pad[:, CH * E:][:, bass.ts(blk, CH * E)].rearrange("p (i e) -> p i e", i=CH)
                        passing()
                        nc.vector.tensor_copy(part_ap(0), comb).then_inc(ffn["split"], 1)
                        done("split", 0)
                        nc.vector.tensor_tensor(pr, comb, part_ap(0), ALU.subtract).then_inc(ffn["split"], 1)
                        done("split", 1)
                        passing()
                        nc.vector.tensor_copy(part_ap(1), pr).then_inc(ffn["split"], 1)
                        done("split", 2)
                        nc.vector.tensor_tensor(pr, pr, part_ap(1), ALU.subtract).then_inc(ffn["split"], 1)
                        done("split", 3)
                        passing()
                        nc.vector.tensor_copy(part_ap(2), pr).then_inc(ffn["fetched"], 1)
                    if t == "C":
                        done("parts_tr", i)
                        done("routed", -1)
                        nc.vector.tensor_copy(cT_route, bank_z[:, 0:BLK // 2].bitcast(BF16)).then_inc(ffn["cT_ready"], 1)
                    if t == "X":
                        done("y_tr", -1)
                        done("stored", -2, 16)
                        nc.vector.scalar_tensor_tensor(res, bank_z[:, :], tg[:, 1:2], x_pad[:, bass.ts(blk, BLK)],
                                                       ALU.mult, ALU.add).then_inc(ffn["y_out"], 1)

                fturns(dve, "dve", ffn_do)

            @block.gpsimd
            def _(pool):
                prologue_pool(pool)
                pool.sem_inc(ready, 1)
                pool.wait_ge(ready, 5)

                def do(blk, done, t, n):
                    if t == "C":
                        done("rsum_ready", n)
                        j = n % PSLOT
                        nc.gpsimd.tensor_tensor(probs[:, j, :], probs[:, j, :], rsum[:, j:j + 1].to_broadcast([P, T]),
                                                ALU.mult).then_inc(att["normed"], 1)
                    if t == "R":
                        done("var_done", n)
                        done("ln2_done", n - 1)
                        nc.gpsimd.tensor_tensor(ln_rstd[:, :], ln_var[:, :], minus_half[:, 0:CH], ALU.pow).then_inc(att["rstd_done"], 1)

                def up_low():
                    over(pool, "transposed")
                    nc.gpsimd.memset(parts_blk, 0.0).then_inc(mid["r_zero"], 1)
                    over(pool, "weighed")
                    nc.gpsimd.memset(wd_raw[:, NJ - 1, :], 0.0).then_inc(mid["wd_pad"], 1)
                    pool.wait_ge(mid["gu_hi"], 2)
                    nc.gpsimd.tensor_tensor(gu_w[1][:, 1, :], raw_gu[:, 1, :], gu_w[1][:, 0, :].bitcast(F32),
                                            ALU.subtract).then_inc(mid["gu_lo"], 1)

                turns(pool, pool_turn, do, before={("R", -1): up_low})
                pool.wait_ge(mid["wd_hi"], 1)
                nc.gpsimd.tensor_tensor(wd_parts[1], wd_raw, wd_parts[0].bitcast(F32),
                                        ALU.subtract).then_inc(mid["wd_lo"], 1)
                pool.wait_ge(mid["wd_lo"], 1)
                pool.wait_ge(mid["sel_done"], 1)
                pool.wait_ge(mid["gu_lo"], 2)

                def ffn_do(blk, done, t, i):
                    done("hid_hi", i)
                    freed(done, "down", i)
                    nc.gpsimd.tensor_tensor(hid_parts[:, slot(i), 1, :], hid[:, slot(i), :],
                                            hid_parts[:, slot(i), 0, :].bitcast(F32), ALU.subtract).then_inc(ffn["hid_lo"], 1)

                fturns(pool, "pool", ffn_do)


_INS = ['x', 'ctx_1024', 'g_xattn', 'g_ffn', 'L0_xattn_wq_w', 'L0_xattn_wq_b', 'L0_xattn_wk_w', 'L0_xattn_wk_b',
        'L0_xattn_wv_w', 'L0_xattn_wv_b', 'L0_xattn_mk', 'L0_xattn_mv', 'L0_xattn_wo_w', 'L0_xattn_wo_b',
        'L0_ffn_gate_w', 'L0_ffn_w_gate', 'L0_ffn_w_up', 'L0_ffn_w_down', 'L0_ffn_sw_gate', 'L0_ffn_sw_up',
        'L0_ffn_sw_down']


def _constants():
    identity = np.eye(P, dtype=np.float32)
    selector = np.zeros((P, NJE, P), dtype=np.float32)
    expert = np.arange(FEX).reshape(NJE, P) // FE
    for part in range(3):
        for e in range(E):
            selector[part * PART + e] = expert == e
    iota = np.tile(np.arange(E, dtype=np.float32), (P, 1))
    return {"identity": identity, "selector": selector, "iota": iota}


def kernel(**inputs):
    import concourse.bacc as _bacc
    from concourse import mybir as _mybir
    from concourse.bass_utils import run_bass_kernel_spmd as _run

    nc = _bacc.Bacc("TRN2", target_bir_lowering=False, num_devices=1)
    arrays, args = {}, []
    named = [(n, np.ascontiguousarray(inputs[n])) for n in _INS] + list(_constants().items())
    for name, arr in named:
        arrays[f"in_{name}"] = arr
        args.append(nc.dram_tensor(f"in_{name}", arr.shape, _mybir.dt.from_np(arr.dtype), kind="ExternalInput").ap())
    out = nc.dram_tensor("out_0", (B, S, D), _mybir.dt.float32, kind="ExternalOutput").ap()
    flamingo_block(nc, *args, out)
    r = _run(nc, [arrays], core_ids=[0])
    return r.results[0]["out_0"]
```
